# Optimizing a Trainium2 kernel written in Bass

```python
import numpy as np
import jax
import jax.numpy as jnp

def _softmax(x, axis=-1):
    return jax.nn.softmax(x, axis=axis)

def _gelu(x):
    return jax.nn.gelu(x, approximate=True)

def _silu(x):
    return jax.nn.silu(x)

def _sigmoid(x):
    return jax.nn.sigmoid(x)

def _layernorm(x, axis=-1, eps=1e-05):
    m = jnp.mean(x, axis=axis, keepdims=True)
    v = jnp.var(x, axis=axis, keepdims=True)
    return (x - m) / jnp.sqrt(v + eps)

def _scatter_add(tgt, idx, src, axis=0):
    return tgt.at[idx].add(src)

def _segment_sum(src, seg, n):
    return jax.ops.segment_sum(src, seg, n)
kernel_name = 'mk_xattn_ffn_d1_seqx_r8_da9ce2'

def setup_inputs(seed: int=0):
    np.random.seed(seed)
    _w = jnp.asarray

    def _rec_inputs():
        import jax
        import jax.numpy as jnp
        _rk = jax.random.key(seed)
        x = -0.0002928 + 1 * jax.random.normal(jax.random.fold_in(_rk, 1), (16, 64, 128), jnp.float32)
        _lenS = 64 - jax.random.randint(jax.random.fold_in(_rk, 7), (16,), 0, max(1, 64 // 4) + 1, jnp.int32)
        _lenS2 = 64 - jax.random.randint(jax.random.fold_in(_rk, 8), (16,), 0, max(1, 64 // 4) + 1, jnp.int32)
        _ctx_1024P = jax.random.normal(jax.random.fold_in(_rk, 11), (16, 16, 128), jnp.float32)
        _ctx_1024c = jax.random.dirichlet(jax.random.fold_in(_rk, 511), 0.3 * jnp.ones((16,), jnp.float32), (16, 64))
        _ctx_1024t = jnp.einsum('bsk,bkd->bsd', _ctx_1024c, _ctx_1024P)
        _ctx_1024t = _ctx_1024t * jax.lax.rsqrt(jnp.mean(jnp.square(_ctx_1024t)) + 1e-12) * 0.953939
        ctx_1024 = -1.39393e-06 + 0.999914 * (_ctx_1024t + 0.3 * jax.random.normal(jax.random.fold_in(_rk, 611), (16, 64, 128), jnp.float32))
        return (x, ctx_1024)
    x, ctx_1024 = _rec_inputs()

    def _L0_xattn_setup():
        import jax, jax.numpy as jnp
        import numpy as np
        EPS = 1e-06
        LN_EPS = 1e-06

        def _mlstm_parallel_stabilized(q, k, v, igate_preact, fgate_preact):
            B, NH, S, DH = q.shape
            log_fg = jax.nn.log_sigmoid(fgate_preact[..., 0])
            cs = jnp.cumsum(log_fg, axis=-1)
            fg_mat = cs[..., :, None] - cs[..., None, :]
            mask = jnp.tril(jnp.ones((S, S), dtype=bool))
            log_D = jnp.where(mask, fg_mat + igate_preact[..., 0][..., None, :], -jnp.inf)
            max_log_D = jnp.max(log_D, axis=-1, keepdims=True)
            D = jnp.exp(log_D - max_log_D)
            k_scaled = k / jnp.sqrt(jnp.float32(DH)).astype(k.dtype)
            qk = jnp.einsum('bhsd,bhtd->bhst', q, k_scaled)
            C = qk * D
            normalizer = jnp.maximum(jnp.abs(jnp.sum(C, axis=-1, keepdims=True)), jnp.exp(-max_log_D))
            C_norm = C / (normalizer + EPS)
            return jnp.einsum('bhst,bhtd->bhsd', C_norm, v)

        def _multihead_layernorm(x, weight):
            mu = jnp.mean(x, axis=-1, keepdims=True)
            var = jnp.mean(jnp.square(x - mu), axis=-1, keepdims=True)
            xn = (x - mu) * jax.lax.rsqrt(var + LN_EPS)
            return xn * weight[None, :, None, :]
        key = jax.random.key(seed)
        ks = jax.random.split(key, 6)
        B, S, E, NH = (2, 256, 128, 8)
        q = jax.random.normal(ks[0], (B, S, E), dtype=jnp.float32)
        k = jax.random.normal(ks[1], (B, S, E), dtype=jnp.float32)
        v = jax.random.normal(ks[2], (B, S, E), dtype=jnp.float32)
        igate_kernel = jnp.zeros((3 * E, NH), dtype=jnp.float32)
        igate_bias = 0.1 * jax.random.normal(ks[3], (NH,), dtype=jnp.float32)
        fgate_kernel = jnp.zeros((3 * E, NH), dtype=jnp.float32)
        fgate_bias = jnp.linspace(3.0, 6.0, NH, dtype=jnp.float32)
        outnorm_weight = jnp.ones((NH, E // NH), dtype=jnp.float32)
        return {'q': q, 'k': k, 'v': v, 'igate_kernel': igate_kernel, 'igate_bias': igate_bias, 'fgate_kernel': fgate_kernel, 'fgate_bias': fgate_bias, 'outnorm_weight': outnorm_weight}
    _L0_xattn_all = _L0_xattn_setup()
    _L0_xattn_in = {k: v for k, v in _L0_xattn_all.items() if k in ('igate_kernel', 'igate_bias', 'fgate_kernel', 'fgate_bias', 'outnorm_weight')}
    del _L0_xattn_all

    def _L0_ffn_setup():
        import jax, jax.numpy as jnp
        import numpy as np
        TOP_K = 2
        EPS = 1e-05

        def layer_norm(x, g, b):
            mu = jnp.mean(x, axis=-1, keepdims=True)
            var = jnp.mean(jnp.square(x - mu), axis=-1, keepdims=True)
            return (x - mu) * jax.lax.rsqrt(var + EPS) * g + b
        key = jax.random.key(seed)
        ks = jax.random.split(key, 12)
        B, S, D, F, E = (2, 256, 128, 512, 8)
        std = 0.02
        return {'x': jax.random.normal(ks[0], (B, S, D), jnp.float32), 'g1': jnp.ones((D,), jnp.float32), 'be1': jnp.zeros((D,), jnp.float32), 'mix_w': jax.random.normal(ks[1], (D, D), jnp.float32) * std, 'mix_b': jnp.zeros((D,), jnp.float32), 'g2': jnp.ones((D,), jnp.float32), 'be2': jnp.zeros((D,), jnp.float32), 'router_w': jax.random.normal(ks[2], (D, E), jnp.float32) * std, 'w1': jax.random.normal(ks[3], (E, D, F), jnp.float32) * std, 'b1': jnp.zeros((E, F), jnp.float32), 'w2': jax.random.normal(ks[4], (E, F, D), jnp.float32) * std, 'b2': jnp.zeros((E, D), jnp.float32)}
    _L0_ffn_all = _L0_ffn_setup()
    _L0_ffn_in = {k: v for k, v in _L0_ffn_all.items() if k in ('g1', 'be1', 'mix_w', 'mix_b', 'g2', 'be2', 'router_w', 'w1', 'b1', 'w2', 'b2')}
    del _L0_ffn_all
    return {'x': x, 'ctx_1024': ctx_1024, 'L0_xattn_igate_kernel': _L0_xattn_in['igate_kernel'], 'L0_xattn_igate_bias': _L0_xattn_in['igate_bias'], 'L0_xattn_fgate_kernel': _L0_xattn_in['fgate_kernel'], 'L0_xattn_fgate_bias': _L0_xattn_in['fgate_bias'], 'L0_xattn_outnorm_weight': _L0_xattn_in['outnorm_weight'], 'L0_ffn_g1': _L0_ffn_in['g1'], 'L0_ffn_be1': _L0_ffn_in['be1'], 'L0_ffn_mix_w': _L0_ffn_in['mix_w'], 'L0_ffn_mix_b': _L0_ffn_in['mix_b'], 'L0_ffn_g2': _L0_ffn_in['g2'], 'L0_ffn_be2': _L0_ffn_in['be2'], 'L0_ffn_router_w': _L0_ffn_in['router_w'], 'L0_ffn_w1': _L0_ffn_in['w1'], 'L0_ffn_b1': _L0_ffn_in['b1'], 'L0_ffn_w2': _L0_ffn_in['w2'], 'L0_ffn_b2': _L0_ffn_in['b2']}

def reference(x, ctx_1024, L0_xattn_igate_kernel, L0_xattn_igate_bias, L0_xattn_fgate_kernel, L0_xattn_fgate_bias, L0_xattn_outnorm_weight, L0_ffn_g1, L0_ffn_be1, L0_ffn_mix_w, L0_ffn_mix_b, L0_ffn_g2, L0_ffn_be2, L0_ffn_router_w, L0_ffn_w1, L0_ffn_b1, L0_ffn_w2, L0_ffn_b2):
    import jax
    import jax.numpy as jnp

    def _L0_xattn_ref(q, k, v, igate_kernel, igate_bias, fgate_kernel, fgate_bias, outnorm_weight):
        import jax, jax.numpy as jnp
        import numpy as np
        EPS = 1e-06
        LN_EPS = 1e-06

        def _mlstm_parallel_stabilized(q, k, v, igate_preact, fgate_preact):
            B, NH, S, DH = q.shape
            log_fg = jax.nn.log_sigmoid(fgate_preact[..., 0])
            cs = jnp.cumsum(log_fg, axis=-1)
            fg_mat = cs[..., :, None] - cs[..., None, :]
            mask = jnp.tril(jnp.ones((S, S), dtype=bool))
            log_D = jnp.where(mask, fg_mat + igate_preact[..., 0][..., None, :], -jnp.inf)
            max_log_D = jnp.max(log_D, axis=-1, keepdims=True)
            D = jnp.exp(log_D - max_log_D)
            k_scaled = k / jnp.sqrt(jnp.float32(DH)).astype(k.dtype)
            qk = jnp.einsum('bhsd,bhtd->bhst', q, k_scaled)
            C = qk * D
            normalizer = jnp.maximum(jnp.abs(jnp.sum(C, axis=-1, keepdims=True)), jnp.exp(-max_log_D))
            C_norm = C / (normalizer + EPS)
            return jnp.einsum('bhst,bhtd->bhsd', C_norm, v)

        def _multihead_layernorm(x, weight):
            mu = jnp.mean(x, axis=-1, keepdims=True)
            var = jnp.mean(jnp.square(x - mu), axis=-1, keepdims=True)
            xn = (x - mu) * jax.lax.rsqrt(var + LN_EPS)
            return xn * weight[None, :, None, :]
        B, S, E = q.shape
        NH = igate_bias.shape[0]
        qkv = jnp.concatenate([q, k, v], axis=-1)
        igate_preact = qkv @ igate_kernel + igate_bias
        fgate_preact = qkv @ fgate_kernel + fgate_bias
        qh = q.reshape(B, S, NH, -1).transpose(0, 2, 1, 3)
        kh = k.reshape(B, S, NH, -1).transpose(0, 2, 1, 3)
        vh = v.reshape(B, S, NH, -1).transpose(0, 2, 1, 3)
        ig = igate_preact.transpose(0, 2, 1)[..., None]
        fg = fgate_preact.transpose(0, 2, 1)[..., None]
        h = _mlstm_parallel_stabilized(qh, kh, vh, ig, fg)
        h_norm = _multihead_layernorm(h, outnorm_weight)
        return h_norm.transpose(0, 2, 1, 3).reshape(B, S, -1)

    def _L0_ffn_ref(x, g1, be1, mix_w, mix_b, g2, be2, router_w, w1, b1, w2, b2):
        import jax, jax.numpy as jnp
        import numpy as np
        TOP_K = 2
        EPS = 1e-05

        def layer_norm(x, g, b):
            mu = jnp.mean(x, axis=-1, keepdims=True)
            var = jnp.mean(jnp.square(x - mu), axis=-1, keepdims=True)
            return (x - mu) * jax.lax.rsqrt(var + EPS) * g + b
        res = x
        n = layer_norm(x, g1, be1)
        x = res + n + (n @ mix_w + mix_b)
        res = x
        n = layer_norm(x, g2, be2)
        B, S, D = n.shape
        E = w1.shape[0]
        flat = n.reshape(-1, D)
        probs = jax.nn.softmax(flat @ router_w, axis=-1)
        topw, topi = jax.lax.top_k(probs, TOP_K)
        combine = jnp.sum(jax.nn.one_hot(topi, E, dtype=flat.dtype) * topw[..., None], axis=1)
        h = jax.nn.silu(jnp.einsum('td,edf->tef', flat, w1) + b1)
        y = jnp.einsum('tef,efd->ted', h, w2) + b2
        out = jnp.einsum('te,ted->td', combine, y)
        return res + out.reshape(B, S, D)
    x = x + _L0_xattn_ref(_layernorm(x, axis=-1), ctx_1024, ctx_1024, L0_xattn_igate_kernel, L0_xattn_igate_bias, L0_xattn_fgate_kernel, L0_xattn_fgate_bias, L0_xattn_outnorm_weight)
    x = x + _L0_ffn_ref(_layernorm(x, axis=-1), L0_ffn_g1, L0_ffn_be1, L0_ffn_mix_w, L0_ffn_mix_b, L0_ffn_g2, L0_ffn_be2, L0_ffn_router_w, L0_ffn_w1, L0_ffn_b1, L0_ffn_w2, L0_ffn_b2)
    return x

_drawn_inputs = setup_inputs


def setup_inputs(seed=0):
    import zlib

    import numpy as np

    out = dict(_drawn_inputs(seed))
    spreads = {'L0_xattn_igate_kernel': (0.0, 0.1),
     'L0_xattn_fgate_kernel': (0.0, 0.1),
     'L0_xattn_outnorm_weight': (1.0, 0.2),
     'L0_ffn_g1': (1.0, 0.2),
     'L0_ffn_be1': (0.0, 0.269),
     'L0_ffn_mix_b': (0.0, 0.291),
     'L0_ffn_g2': (1.0, 0.6),
     'L0_ffn_be2': (0.0, 0.8),
     'L0_ffn_b1': (0.0, 0.8),
     'L0_ffn_b2': (0.0, 0.8)}
    factors = {'L0_xattn_igate_bias': 47.212, 'L0_ffn_router_w': 8.0, 'L0_ffn_w1': 8.0, 'L0_ffn_w2': 8.0}
    for name, (base, spread) in spreads.items():
        noise = np.random.default_rng([zlib.crc32(name.encode()), seed]).standard_normal(out[name].shape)
        drawn = base * np.exp(spread * noise) if base else spread * noise
        out[name] = jnp.asarray(drawn.astype(out[name].dtype))
    for name, factor in factors.items():
        out[name] = (out[name] * factor).astype(out[name].dtype)
    return out
```

```python
from contextlib import ExitStack

import concourse.bass as bass
from concourse import mybir

ALU = mybir.AluOpType
ACT = mybir.ActivationFunctionType
AX = mybir.AxisListType
F32 = mybir.dt.float32
F32R = mybir.dt.float32r
BF16 = mybir.dt.bfloat16

B, S, E, NH = 16, 64, 128, 8
DH = E // NH
NT = B * S // 128
NX, F = 8, 512
FC = F // 128
TOK = B * S
NEG = -1.0e30
LOWEST = -3.0e38
ORDER = [jp * (NT // 2) + jh for jh in range(NT // 2) for jp in range(2)]


class Steps:

    def __init__(self, engine, sem):
        self.engine, self.sem, self.n = engine, sem, 0

    def mark(self, instruction):
        instruction.then_inc(self.sem, 1)
        self.n += 1

    def wait(self):
        self.engine.wait_ge(self.sem, self.n)

    def then(self, instruction):
        self.mark(instruction)
        self.wait()


def build(nc, x, ctx_in, ig_k, ig_b, fg_k, fg_b, onorm_w, g1, be1, mix_w, mix_b, g2, be2,
          router_w, w1, b1, w2, b2, out):
    stack = ExitStack()
    with stack:
        def sb(name, shape, dt=F32):
            return stack.enter_context(nc.sbuf_tensor(name, shape, dt))

        def sem(name):
            return stack.enter_context(nc.semaphore(name))

        ident = sb("ident", [128, 128])
        ident_r = sb("ident_r", [128, 128], F32R)
        ident_bf = sb("ident_bf", [128, 128], BF16)
        eye2 = sb("eye2", [128, S])
        tri = sb("tri", [128, 128])
        later_bf = sb("later_bf", [128, S], BF16)
        pick = sb("pick", [128, NT, 2, S])
        pick_r = sb("pick_r", [128, NT, 2, S], F32R)
        head_of_row = sb("head_of_row", [128, NH, 16])
        h8 = sb("h8", [128, NH])
        e8 = sb("e8", [128, NH])
        e4 = sb("e4", [128, NH // 2])
        zeros = sb("zeros", [128, S])
        minus_half = sb("minus_half", [128, 32])
        rank = sb("rank", [128, NX])
        ones_row = sb("ones_row", [1, 128])
        comb_all = sb("comb_all", [128, NX, TOK])
        x1 = comb_all[:, 0].rearrange("p (j e) -> p j e", e=E)
        cx = comb_all[:, 1].rearrange("p (j e) -> p j e", e=E)
        qn = comb_all[:, 2].rearrange("p (j e) -> p j e", e=E)
        q_t = comb_all[:, 3].rearrange("p (j b t) -> p j b t", b=2, t=S)
        k_m = comb_all[:, 4:6].rearrange("p a (j g b t) -> p (a j) g b t", g=2, b=2, t=S)
        qd = comb_all[:, 6:8].rearrange("p a (r g h s) -> p (a r) g h s", r=2, g=2, s=S)
        x2 = sb("x2", [128, NT, E])
        wg = sb("wg", [128, 3, 2, 16])
        wq = sb("wq", [128, 2, 16])
        wc = sb("wc", [128, 2, 16])
        gbias = sb("gbias", [128, 16])
        onw = sb("onw", [128, E])
        vecs = sb("vecs", [36, 128])
        vecs_t = sb("vecs_t", [128, 36])
        mixw = sb("mixw", [128, E])
        mixb = sb("mixb", [1, E])
        rw = sb("rw", [128, NX])
        b2s = sb("b2s", [NX, E])
        stats = sb("stats", [128, NT, 6])
        mv = sb("mv", [128, NT, 2])
        rstd = sb("rstd", [128, NT])
        v2 = sb("v2", [128, NT, NH, 2, DH + 1])
        gates = sb("gates", [128, NT, 16])
        absf = sb("absf", [128, NT, NH])
        ef = sb("ef", [128, NT, NH])
        lnf = sb("lnf", [128, NT, NH])
        logf = sb("logf", [128, NT, NH])
        a_tok = sb("a_tok", [128, NT * NH])
        a_hi = sb("a_hi", [128, NT * NH], F32R)
        a_lo = sb("a_lo", [128, NT * NH], F32R)
        a_blk = sb("a_blk", [128, 2, NT * NH])
        c_blk = sb("c_blk", [128, 2, NT * NH])
        top_a = sb("top_a", [128, S])
        top_hi = sb("top_hi", [128, S], F32R)
        top_lo = sb("top_lo", [128, S], F32R)
        m_full = sb("m_full", [128, S])
        topx_hi = sb("topx_hi", [128, NH, S], F32R)
        topx_lo = sb("topx_lo", [128, NH, S], F32R)
        em = sb("em", [128, 4, 2, NH])
        dec = sb("dec", [128, 2, NH * S])
        cmat = sb("cmat", [128, 2, NH, S])
        t1 = sb("t1", [128, 2, 32])
        nrm = sb("nrm", [128, 2, 32])
        rn = sb("rn", [128, 2, 32])
        s16 = sb("s16", [128, 2, 32])
        mu = sb("mu", [128, 2, 32])
        uc = sb("uc", [128, 2, 4 * E])
        usq = sb("usq", [128, 2, 4 * E])
        v16 = sb("v16", [128, 2, 32])
        rn2 = sb("rn2", [128, 2, 32])
        hv = sb("hv", [128, 2, 32])
        hve = sb("hve", [128, 2, 32])
        hr = sb("hr", [128, 2, 32])
        hf = sb("hf", [128, 2, 32])
        h_f = sb("h_f", [128, 2, TOK])
        att = h_f[:, 0].rearrange("p (t e) -> p t e", e=E)
        attw = h_f[:, 1].rearrange("p (t e) -> p t e", e=E)
        x_mid = sb("x_mid", [128, NT, E])
        st1 = sb("st1", [128, NT, 6])
        mv1 = sb("mv1", [128, NT, 2])
        ve1 = sb("ve1", [128, NT])
        r1 = sb("r1", [128, NT])
        r1sq = sb("r1sq", [128, NT])
        vn = sb("vn", [128, NT])
        r1b = sb("r1b", [128, NT])
        y0 = sb("y0", [128, NT, E])
        nrow = sb("nrow", [128, NT, E])
        n_t = sb("n_t", [128, TOK])
        z = sb("z", [128, NT, E])
        st2 = sb("st2", [128, NT, 6])
        mv2 = sb("mv2", [128, NT, 2])
        ve2 = sb("ve2", [128, NT])
        r2 = sb("r2", [128, NT])
        zn = sb("zn", [128, NT, E])
        base = sb("base", [128, NT, E])
        n2 = sb("n2", [128, TOK])
        n2_hi = sb("n2_hi", [128, TOK], F32R)
        n2_lo = sb("n2_lo", [128, TOK], F32R)
        rsm = sb("rsm", [128, 8, NT])
        rt = sb("rt", [128, 12, NT, NX])
        comb = sb("comb", [128, NT, NX])
        comb_t = sb("comb_t", [NX, TOK])
        raw = sb("raw", [128, 2, 2 * F])
        part = uc[:].rearrange("p a n -> p (a n)")
        acc = usq[:].rearrange("p a n -> p (a n)")
        base_b = nrow
        fin = y0
        w_hi = sb("w_hi", [128, 2, 2 * F], F32R)
        w_lo = sb("w_lo", [128, 2, 2 * F], F32R)
        b1_now = sb("b1_now", [128, 2, FC])
        h_hi = sb("h_hi", [128, 4, TOK], F32R)
        h_lo = sb("h_lo", [128, 4, TOK], F32R)
        comb_dram = nc.dram_tensor("comb_dram", (NX, TOK), F32, kind="Internal").ap()

        ps = stack.enter_context(nc.psum_tensor("ps", [128, 8, 512], F32))

        names = (
            "ld_x ld_ctx ld_gate ld_x2 ld_onw ld_vecs ld_mix ld_rw ld_raw0 ld_raw1 comb_out comb_in "
            "out_done c_pool c_ident c_identr c_pick c_masks c_v2zero c_small c_blkzero c_kzero "
            "p_rstd p_head p_ln1 p_ln2 v_wq "
            "v_stats v_q v_logf v_chain v_gates v_absf v_a v_ahl v_scan v_topx v_m v_qd v_c v_small v_h8 v_wc "
            "v_rn v_uc v_v16 v_mv1 v_nrow v_mv2 v_zn v_n2lo v_rt v_comb v_lo v_comb_e v_whi v_b1 p_wlo v_base v_fin "
            "a_k a_q a_v2 a_exp a_ln a_cblk a_em a_dec a_usq a_nt a_n2 a_rexp a_combt a_h a_hi a_vecs a_id "
            "t_ctx t_q t_gates t_cs t_at t_ct t_em t_vecs t_l t_qk t_pv t_nrow t_z t_n2 t_router t_combt t_b2 "
            "t_up t_down t_fin"
        ).split()
        s = {n: sem(n) for n in names}
        ld_raw = [s["ld_raw0"], s["ld_raw1"]]

        def u_half(half):
            v = ps[:, 4 + 2 * half:6 + 2 * half, 0:2 * NH * (DH + 1)]
            return v.rearrange("p j (c d) -> p j c d", d=DH + 1)

        blk = (stack.enter_context(nc.Block()))
        xv = x.rearrange("(j b) s (g e) -> b s j g e", b=2, g=2)
        cv = ctx_in.rearrange("(j b) s (g e) -> b s j g e", b=2, g=2)
        x1v = x1.rearrange("p j (g e) -> p j g e", g=2)
        cxv = cx.rearrange("p j (g e) -> p j g e", g=2)
        x2v = x.rearrange("(jp t) s e -> jp s t e", jp=2)
        outv = out.rearrange("(jp t) s e -> jp s t e", jp=2)

        def load_raw(eng, e, slot):
            if isinstance(e, int):
                a, b = w1[e], w2[e]
            else:
                a, b = w1[bass.ds(e, 1), :, :].squeeze(0), w2[bass.ds(e, 1), :, :].squeeze(0)
            eng.dma_start(raw[:, slot, 0:F], a).then_inc(ld_raw[slot], 16)
            eng.dma_start(raw[:, slot, F:2 * F].rearrange("p (c d) -> p c d", c=FC),
                          b.rearrange("(c p) d -> p c d", p=128)).then_inc(ld_raw[slot], 16)

        @blk.sync
        def _(sp):
            sp.dma_start(x1v[0:64], xv[0]).then_inc(s["ld_x"], 16)
            for g in range(2):
                sp.dma_start(x1v[64:128, :, 1 - g], xv[1, :, :, g]).then_inc(s["ld_x"], 16)
            for half in range(2):
                for n, kern in ((0, fg_k), (1, ig_k)):
                    sp.dma_start(wg[64 * half:64 * half + 64, :, :, 8 * n:8 * n + 8],
                                 kern.rearrange("(c g r) h -> r c g h", c=3, g=2)).then_inc(s["ld_gate"], 16)
            for n, bias in ((0, fg_b), (1, ig_b)):
                sp.dma_start(gbias[:, 8 * n:8 * n + 8],
                             bias.rearrange("(a h) -> a h", a=1).to_broadcast([128, NH])).then_inc(s["ld_gate"], 16)
            for jp in range(2):
                sp.dma_start(x2[64 * jp:64 * jp + 64], x2v[jp]).then_inc(s["ld_x2"], 16)
            sp.dma_start(onw[:], onorm_w.rearrange("h d -> (h d)").rearrange("(a n) -> a n", a=1)
                         .to_broadcast([128, E])).then_inc(s["ld_onw"], 16)
            sp.dma_start(mixw[:], mix_w).then_inc(s["ld_mix"], 16)
            sp.dma_start(mixb[:], mix_b.rearrange("(a n) -> a n", a=1)).then_inc(s["ld_mix"], 16)
            sp.dma_start(rw[:], router_w).then_inc(s["ld_rw"], 16)
            sp.dma_start(b2s[:], b2).then_inc(s["ld_rw"], 16)
            load_raw(sp, 0, 0)
            load_raw(sp, 1, 1)
            sp.wait_ge(s["a_combt"], 2)
            sp.dma_start(comb_dram, comb_t[:]).then_inc(s["comb_out"], 16)
            sp.wait_ge(s["comb_out"], 16)
            for half in range(2):
                sp.dma_start(comb_all[:, 4 * half:4 * half + 4, :],
                             comb_dram[4 * half:4 * half + 4, :].rearrange("(a e) t -> a e t", a=1)
                             .to_broadcast([128, 4, TOK])).then_inc(s["comb_in"], 16)
            with sp.Fori(1, NX // 2) as i:
                for slot in range(2):
                    sp.wait_ge(s["v_whi"], 2 * i + slot - 1)
                    sp.wait_ge(s["p_wlo"], 2 * i + slot - 1)
                    load_raw(sp, 2 * i + slot, slot)
            sp.wait_ge(s["v_fin"], 2)
            for jp in range(2):
                sp.dma_start(outv[jp], fin[64 * jp:64 * jp + 64]).then_inc(s["out_done"], 16)
            sp.wait_ge(s["out_done"], 32)

        @blk.gpsimd
        def _(pool):
            k = Steps(pool, s["c_pool"])
            k.then(pool.memset(ident[:], 0.0))
            pool.affine_select(out=ident[:], in_=ident[:], compare_op=ALU.not_equal, fill=1.0, base=0,
                               pattern=[[-1, 128]], channel_multiplier=1).then_inc(s["c_ident"], 1)
            for t in (tri, pick, e8, head_of_row):
                k.mark(pool.memset(t[:], 1.0))
            k.mark(pool.memset(later_bf[:], 0.0))
            k.wait()
            pool.wait_ge(s["c_ident"], 1)
            pool.tensor_tensor(eye2[:], ident[:, 0:S], ident[:, S:128], ALU.add).then_inc(s["c_small"], 1)
            k.then(pool.affine_select(out=tri[:], in_=tri[:], compare_op=ALU.is_ge, fill=0.0, base=0,
                                      pattern=[[1, 128]], channel_multiplier=-1))
            pool.memset(tri[0:64, 64:128], 0.0).then_inc(s["c_small"], 1)
            pool.wait_ge(s["c_small"], 2)
            k.then(pool.affine_select(out=e8[:], in_=e8[:], compare_op=ALU.is_ge, fill=0.0, base=0,
                                      pattern=[[-DH, NH]], channel_multiplier=1))
            k.then(pool.affine_select(out=e8[:], in_=e8[:], compare_op=ALU.is_ge, fill=0.0, base=DH - 1,
                                      pattern=[[DH, NH]], channel_multiplier=-1))
            k.then(pool.tensor_scalar(e8[:], e8[:], DH ** -0.5, None, ALU.mult))
            pool.tensor_tensor(e4[:], e8[:, 0:4], e8[:, 4:8], ALU.add).then_inc(s["c_small"], 1)
            pool.wait_ge(s["v_stats"], 2 * NT)
            pool.wait_ge(s["v_small"], 4)
            k.then(pool.tensor_scalar(rstd[:], mv[:, :, 1], 1e-5, None, ALU.add))
            pool.tensor_tensor(rstd[:], rstd[:], minus_half[:, 0:NT], ALU.pow).then_inc(s["p_rstd"], 1)
            pool.wait_ge(s["p_rstd"], 1)
            pool.affine_select(out=head_of_row[:], in_=head_of_row[:], compare_op=ALU.is_equal, fill=0.0, base=0,
                               pattern=[[-1, NH], [-NH, 16]], channel_multiplier=1).then_inc(s["c_masks"], 1)
            pool.wait_ge(s["c_masks"], 1)
            for b in range(2):
                pool.affine_select(out=later_bf[64 * b:64 * b + 64], in_=later_bf[64 * b:64 * b + 64],
                                   compare_op=ALU.is_ge, fill=NEG, base=0,
                                   pattern=[[1, S]], channel_multiplier=-1).then_inc(s["c_masks"], 1)
                pool.wait_ge(s["c_masks"], b + 2)
            v = pick[:].rearrange("p j b t -> p j b t")
            k.then(pool.affine_select(out=v, in_=v, compare_op=ALU.is_ge, fill=0.0, base=0,
                                      pattern=[[-NH, NT], [-64, 2], [0, S]], channel_multiplier=1))
            pool.affine_select(out=v, in_=v, compare_op=ALU.is_ge, fill=0.0, base=NH - 1,
                               pattern=[[NH, NT], [64, 2], [0, S]], channel_multiplier=-1).then_inc(s["c_pick"], 1)
            for half in range(2):
                pool.wait_ge(s["v_rn"], half + 1)
                k.then(pool.tensor_tensor(rn2[:, half], rn[:, half], rn[:, half], ALU.mult))
                pool.wait_ge(s["v_v16"], half + 1)
                k.then(pool.tensor_tensor(hv[:, half], v16[:, half], rn2[:, half], ALU.mult))
                k.then(pool.tensor_scalar(hve[:, half], hv[:, half], 1.0 / DH, 1e-6, ALU.mult, ALU.add))
                k.then(pool.tensor_tensor(hr[:, half], hve[:, half], minus_half[:], ALU.pow))
                pool.tensor_tensor(hf[:, half], hr[:, half], rn[:, half], ALU.mult).then_inc(s["p_head"], 1)
                h4 = slice(4 * half, 4 * half + 4)
                pool.wait_ge(s["v_mv1"], 8 * (half + 1))
                k.then(pool.tensor_scalar(ve1[:, h4], mv1[:, h4, 1], 1e-5, None, ALU.add))
                pool.tensor_tensor(r1[:, h4], ve1[:, h4], minus_half[:, 0:4], ALU.pow).then_inc(s["p_ln1"], 1)
                pool.wait_ge(s["p_ln1"], 2 * half + 1)
                k.then(pool.tensor_tensor(r1sq[:, h4], r1[:, h4], r1[:, h4], ALU.mult))
                k.then(pool.tensor_tensor(vn[:, h4], mv1[:, h4, 1], r1sq[:, h4], ALU.mult))
                k.then(pool.tensor_scalar(vn[:, h4], vn[:, h4], 1e-5, None, ALU.add))
                pool.tensor_tensor(r1b[:, h4], vn[:, h4], minus_half[:, 0:4], ALU.pow).then_inc(s["p_ln1"], 1)
                pool.wait_ge(s["v_mv2"], 8 * (half + 1))
                k.then(pool.tensor_scalar(ve2[:, h4], mv2[:, h4, 1], 1e-5, None, ALU.add))
                pool.tensor_tensor(r2[:, h4], ve2[:, h4], minus_half[:, 0:4], ALU.pow).then_inc(s["p_ln2"], 1)

            def w_low(e, slot):
                pool.wait_ge(s["v_whi"], e + 1)
                pool.tensor_tensor(w_lo[:, slot, :], raw[:, slot, :], w_hi[:, slot, :].bitcast(F32), ALU.subtract
                                   ).then_inc(s["p_wlo"], 1)
            w_low(0, 0)
            w_low(1, 1)
            with pool.Fori(1, NX // 2) as i:
                for slot in range(2):
                    w_low(2 * i + slot, slot)

        @blk.scalar
        def _(act):
            act.dma_start(cxv[0:64], cv[0]).then_inc(s["ld_ctx"], 16)
            for g in range(2):
                act.dma_start(cxv[64:128, :, 1 - g], cv[1, :, :, g]).then_inc(s["ld_ctx"], 16)
            act.dma_start(vecs[0:32, :], b1.rearrange("e (c f) -> (e c) f", f=128)).then_inc(s["ld_vecs"], 16)
            for n, v in enumerate((g1, be1, g2, be2)):
                act.dma_start(vecs[32 + n:33 + n, :], v.rearrange("(a n) -> a n", a=1)).then_inc(s["ld_vecs"], 16)
            act.wait_ge(s["c_ident"], 1)
            act.activation(ident_r[:], ident[:], ACT.Copy).then_inc(s["a_id"], 1)
            act.activation(ident_bf[:], ident[:], ACT.Copy).then_inc(s["a_id"], 1)
            act.wait_ge(s["t_ctx"], NT)
            act.wait_ge(s["c_kzero"], 1)
            kv = k_m.rearrange("p (a j) g b t -> p a j g b t", a=2)
            pv = ps[:, 2:4, :].rearrange("p a (j b t) -> p a j b t", j=4, b=2)
            for rh in range(2):
                for b in range(2):
                    for a in range(2):
                        act.activation(kv[64 * rh:64 * rh + 64, a, :, rh ^ b, b, :],
                                       pv[64 * rh:64 * rh + 64, a, :, b, :], ACT.Copy).then_inc(s["a_k"], 1)
            for a in range(2):
                act.wait_ge(s["t_q"], 4 * (a + 1))
                act.activation(q_t[:, 4 * a:4 * a + 4].rearrange("p j b t -> p (j b t)"), ps[:, a, :],
                               ACT.Copy).then_inc(s["a_q"], 1)
            act.wait_ge(s["c_v2zero"], 2)
            cb = cx.rearrange("p j (g h d) -> p j g h d", g=2, h=4)
            act.activation(v2[0:64, :, :, 0, 0:DH], cx[0:64].rearrange("p j (h d) -> p j h d", h=NH),
                           ACT.Copy).then_inc(s["a_v2"], 1)
            for g in range(2):
                act.activation(v2[64:128, :, 4 * g:4 * g + 4, 1, 0:DH], cb[64:128, :, 1 - g],
                               ACT.Copy).then_inc(s["a_v2"], 1)
            act.wait_ge(s["c_pick"], 1)
            act.activation(pick_r[:], pick[:], ACT.Copy).then_inc(s["a_id"], 1)
            act.wait_ge(s["v_absf"], 1)
            act.activation(ef[:], absf[:], ACT.Exp, scale=-1.0).then_inc(s["a_exp"], 1)
            act.wait_ge(s["a_exp"], 1)
            act.activation(lnf[:], ef[:], ACT.Ln, bias=1.0).then_inc(s["a_ln"], 1)
            act.wait_ge(s["t_cs"], 1)
            act.wait_ge(s["v_a"], 2)
            act.wait_ge(s["c_blkzero"], 2)
            for b in range(2):
                act.activation(c_blk[64 * b:64 * b + 64, b, :], ps[64 * b:64 * b + 64, 5, 0:64],
                               ACT.Copy).then_inc(s["a_cblk"], 1)
            act.wait_ge(s["t_vecs"], 1)
            act.activation(vecs_t[:], ps[:, 7, 256:292], ACT.Copy).then_inc(s["a_vecs"], 1)

            def decay(j):
                act.wait_ge(s["t_l"], j + 1)
                if j >= 2:
                    act.wait_ge(s["v_c"], j - 1)
                act.activation(dec[:, j % 2, :], ps[:, j % 2, :], ACT.Exp).then_inc(s["a_dec"], 1)
            for j in range(NT):
                decay(j)
                if j == 0:
                    act.wait_ge(s["t_em"], 2)
                    act.activation(em[:].rearrange("p jh b h -> p b jh h"),
                                   ps[:, 6, 128:192].rearrange("p (b jh h) -> p b jh h", b=2, h=NH),
                                   ACT.Exp, scale=-1.0).then_inc(s["a_em"], 1)
            for half in range(2):
                act.wait_ge(s["v_uc"], half + 1)
                act.activation(usq[:, half, :], uc[:, half, :], ACT.Square).then_inc(s["a_usq"], 1)
                cols = slice(512 * half, 512 * half + 512)
                act.wait_ge(s["t_nrow"], 4 * (half + 1))
                act.wait_ge(s["a_vecs"], 1)
                act.activation(n_t[:, cols], ps[:, half, :], ACT.Identity, bias=vecs_t[:, 33:34],
                               scale=vecs_t[:, 32:33]).then_inc(s["a_nt"], 1)
                act.wait_ge(s["t_n2"], 4 * (half + 1))
                act.activation(n2[:, cols], ps[:, half, :], ACT.Identity, bias=vecs_t[:, 35:36],
                               scale=vecs_t[:, 34:35]).then_inc(s["a_n2"], 1)
                act.activation(n2_hi[:, cols], ps[:, half, :], ACT.Identity, bias=vecs_t[:, 35:36],
                               scale=vecs_t[:, 34:35]).then_inc(s["a_n2"], 1)
            act.wait_ge(s["v_rt"], 2)
            act.activation(rt[:, 1], rt[:, 0], ACT.Exp).then_inc(s["a_rexp"], 1)

            def hidden(i, g):
                n, expert = 8 * i + g, 2 * i + g // FC
                first = isinstance(i, int)
                act.wait_ge(s["t_up"], n + 1)
                src = ps[:, 2 * (g % 2):2 * (g % 2) + 2, :].rearrange("p a n -> p (a n)")
                bias = b1_now[:, g // FC % 2, g % FC:g % FC + 1]
                if g % FC == 0:
                    act.wait_ge(s["v_b1"], expert + 1)
                if not (first and n < 2):
                    act.wait_ge(s["v_lo"], n - 1)
                act.activation(h_f[:, g % 2, :], src, ACT.Silu, bias=bias).then_inc(s["a_h"], 1)
                if not (first and n < 4):
                    act.wait_ge(s["t_down"], n - 3)
                act.activation(h_hi[:, g % 4, :], src, ACT.Silu, bias=bias).then_inc(s["a_hi"], 1)

            hidden(0, 0)
            hidden(0, 1)
            for half in range(2):
                act.wait_ge(s["t_combt"], 4 * (half + 1))
                act.activation(comb_t[:, 512 * half:512 * half + 512], ps[0:NX, 4 + half, :], ACT.Copy
                               ).then_inc(s["a_combt"], 1)
            for g in range(2, 8):
                hidden(0, g)
            with act.Fori(1, NX // 2) as i:
                for g in range(8):
                    hidden(i, g)

        @blk.vector
        def _(dve):
            k = Steps(dve, s["v_chain"])
            dve.memset(minus_half[:], -0.5).then_inc(s["v_small"], 1)
            dve.memset(zeros[:], 0.0).then_inc(s["v_small"], 1)
            for e in range(NX):
                m = dve.memset(rank[:, e:e + 1], float(NX - e))
            m.then_inc(s["v_small"], 1)
            dve.memset(ones_row[:], 1.0).then_inc(s["v_small"], 1)
            dve.memset(k_m, 0.0).then_inc(s["c_kzero"], 1)
            dve.wait_ge(s["ld_x"], 48)
            for j in range(NT):
                dve.bn_stats(stats[:, j], x1[:, j]).then_inc(s["v_stats"], 1)
            for j in range(NT):
                dve.wait_ge(s["v_stats"], j + 1)
                dve.bn_aggr(mv[:, j], stats[:, j]).then_inc(s["v_stats"], 1)
            dve.memset(a_blk[:], 0.0).then_inc(s["c_blkzero"], 1)
            dve.memset(c_blk[:], 0.0).then_inc(s["c_blkzero"], 1)
            dve.wait_ge(s["v_stats"], 2 * NT)
            dve.wait_ge(s["p_rstd"], 1)
            for j in range(NT):
                dve.tensor_scalar(qn[:, j], x1[:, j], mv[:, j, 0:1], rstd[:, j:j + 1], ALU.subtract, ALU.mult
                                  ).then_inc(s["v_q"], 1)
            dve.wait_ge(s["ld_gate"], 96)
            dve.tensor_tensor(wc[:], wg[:, 1], wg[:, 2], ALU.add).then_inc(s["v_wc"], 1)
            dve.tensor_copy(wq[0:64, :, :], wg[0:64, 0, :, :]).then_inc(s["v_wq"], 1)
            for b in range(2):
                dve.tensor_copy(wq[64:128, b, :], wg[64:128, 0, 1 - b, :]).then_inc(s["v_wq"], 1)
            dve.memset(v2[:], 0.0).then_inc(s["c_v2zero"], 1)
            dve.wait_ge(s["c_v2zero"], 1)
            for b in range(2):
                m = dve.memset(v2[64 * b:64 * b + 64, :, :, b, DH:DH + 1], 1.0)
            m.then_inc(s["c_v2zero"], 1)
            dve.wait_ge(s["c_masks"], 3)
            dve.tensor_reduce(h8[:], head_of_row[:], axis=AX.X, op=ALU.add).then_inc(s["v_h8"], 1)

            def q_diag(n):
                j = ORDER[n]
                dve.wait_ge(s["a_q"], j // 4 + 1)
                dve.wait_ge(s["c_small"], 3)
                if n >= 4:
                    dve.wait_ge(s["t_qk"], n - 3)
                for rh in range(2):
                    rows = slice(64 * rh, 64 * rh + 64)
                    for g in range(2):
                        dve.tensor_tensor(qd[rows, n % 4, g], q_t[rows, j, rh ^ g, None, :].to_broadcast([64, 4, S]),
                                          e4[rows, :, None].to_broadcast([64, 4, S]), ALU.mult).then_inc(s["v_qd"], 1)
            dve.wait_ge(s["t_gates"], NT)
            dve.tensor_tensor(gates[:], ps[:, 4, 0:128].rearrange("p (j g) -> p j g", g=16),
                              gbias[:, None, :].to_broadcast([128, NT, 16]), ALU.add).then_inc(s["v_gates"], 1)
            dve.wait_ge(s["v_gates"], 1)
            dve.scalar_tensor_tensor(out=absf[:], in0=gates[:, :, 0:8], scalar=-1.0, in1=gates[:, :, 0:8],
                                     op0=ALU.mult, op1=ALU.max).then_inc(s["v_absf"], 1)
            q_diag(0)
            dve.wait_ge(s["a_ln"], 1)
            dve.scalar_tensor_tensor(out=logf[:], in0=gates[:, :, 0:8], scalar=0.0, in1=lnf[:], op0=ALU.min,
                                     op1=ALU.subtract).then_inc(s["v_logf"], 1)
            dve.wait_ge(s["t_cs"], 1)
            for b in range(2):
                rows = slice(64 * b, 64 * b + 64)
                dve.tensor_tensor(a_blk[rows, b].rearrange("p (j h) -> p j h", h=NH), gates[rows, :, 8:16],
                                  ps[rows, 5, 0:64].rearrange("p (j h) -> p j h", h=NH), ALU.subtract
                                  ).then_inc(s["v_a"], 1)
            dve.wait_ge(s["v_a"], 2)
            for b in range(2):
                rows = slice(64 * b, 64 * b + 64)
                dve.tensor_copy(a_hi[rows, :], a_blk[rows, b]).then_inc(s["v_ahl"], 1)
            dve.wait_ge(s["v_ahl"], 2)
            for b in range(2):
                rows = slice(64 * b, 64 * b + 64)
                dve.tensor_tensor(a_lo[rows, :], a_blk[rows, b], a_hi[rows, :].bitcast(F32), ALU.subtract
                                  ).then_inc(s["v_ahl"], 1)
            dve.wait_ge(s["t_at"], 1)
            dve.tensor_tensor_scan(out=top_a[:], data0=zeros[:], data1=ps[:, 6, 0:64], initial=LOWEST,
                                   op0=ALU.add, op1=ALU.max).then_inc(s["v_scan"], 1)
            dve.wait_ge(s["v_scan"], 1)
            k.then(dve.tensor_copy(top_hi[:], top_a[:]))
            k.then(dve.tensor_tensor(top_lo[:], top_a[:], top_hi[:].bitcast(F32), ALU.subtract))
            dve.wait_ge(s["v_h8"], 1)
            for src, dst in ((top_hi, topx_hi), (top_lo, topx_lo)):
                dve.scalar_tensor_tensor(out=dst[:], in0=src[:, None, :].bitcast(F32).to_broadcast([128, NH, S]),
                                         scalar=-1.0, in1=h8[:, :, None].to_broadcast([128, NH, S]),
                                         op0=ALU.mult, op1=ALU.mult).then_inc(s["v_topx"], 1)
            dve.wait_ge(s["t_ct"], 1)
            dve.tensor_tensor(m_full[:], ps[:, 7, 0:64], top_a[:], ALU.add).then_inc(s["v_m"], 1)

            def weigh(j):
                dve.wait_ge(s["t_qk"], j + 1)
                dve.wait_ge(s["a_dec"], j + 1)
                if j >= 2:
                    dve.wait_ge(s["t_pv"], j - 1)
                dve.tensor_tensor(cmat[:, j % 2].rearrange("p h s -> p (h s)"), ps[:, 2 + j % 2, :],
                                  dec[:, j % 2, :], ALU.mult).then_inc(s["v_c"], 1)

            def w_high(e, slot):
                dve.tensor_scalar(b1_now[:, slot, :], vecs_t[:, bass.ds(FC * e, FC)], 1.0, None, ALU.mult
                                  ).then_inc(s["v_b1"], 1)
                dve.wait_ge(ld_raw[slot], e_loaded(e, slot))
                dve.tensor_scalar(w_hi[:, slot, :], raw[:, slot, :], 1.0, None, ALU.mult).then_inc(s["v_whi"], 1)

            def e_loaded(e, slot):
                return (e - slot) * 16 + 32

            q_diag(1)
            for j in range(NT):
                weigh(j)
                if j + 2 < NT:
                    q_diag(j + 2)
            dve.wait_ge(s["a_vecs"], 1)
            w_high(0, 0)
            w_high(1, 1)

            def heads(half):
                u = u_half(half)
                sums = u[:, :, :, DH]
                v = lambda t: t[:, half].rearrange("p (j c) -> p j c", j=2)
                dve.wait_ge(s["t_pv"], 4 * (half + 1))
                dve.wait_ge(s["a_em"], 1)
                emv = em[:, 2 * half:2 * half + 2].rearrange("p j b h -> p j (b h)")
                k.then(dve.scalar_tensor_tensor(out=v(t1), in0=sums, scalar=-1.0, in1=emv,
                                                op0=ALU.mult, op1=ALU.max))
                k.then(dve.tensor_tensor(v(nrm), sums, v(t1), ALU.max))
                k.then(dve.tensor_scalar(nrm[:, half], nrm[:, half], 1e-6, None, ALU.add))
                dve.reciprocal(rn[:, half], nrm[:, half]).then_inc(s["v_rn"], 1)
                k.then(dve.tensor_reduce(v(s16), u[:, :, :, 0:DH], axis=AX.X, op=ALU.add))
                k.then(dve.tensor_scalar(mu[:, half], s16[:, half], 1.0 / DH, None, ALU.mult))
                ucv = uc[:, half].rearrange("p (j c d) -> p j c d", j=2, d=DH)
                dve.tensor_tensor(ucv, u[:, :, :, 0:DH], v(mu)[:, :, :, None].to_broadcast([128, 2, 16, DH]),
                                  ALU.subtract).then_inc(s["v_uc"], 1)
                dve.wait_ge(s["v_uc"], half + 1)
                dve.wait_ge(s["a_usq"], half + 1)
                dve.tensor_reduce(v16[:, half], usq[:, half].rearrange("p (c d) -> p c d", d=DH), axis=AX.X,
                                  op=ALU.add).then_inc(s["v_v16"], 1)
                h4 = slice(4 * half, 4 * half + 4)
                dve.wait_ge(s["p_head"], half + 1)
                k.then(dve.tensor_tensor(att[:, h4].rearrange("p t (h d) -> p (t h) d", d=DH),
                                         uc[:, half].rearrange("p (c d) -> p c d", d=DH),
                                         hf[:, half, :, None].to_broadcast([128, 32, DH]), ALU.mult))
                dve.wait_ge(s["ld_onw"], 16)
                k.then(dve.tensor_tensor(attw[:, h4], att[:, h4], onw[:, None, :].to_broadcast([128, 4, E]),
                                         ALU.mult))
                dve.wait_ge(s["ld_x2"], 32)
                k.then(dve.tensor_tensor(x_mid[:, h4], attw[:, h4], x2[:, h4], ALU.add))
                for t in range(4 * half, 4 * half + 4):
                    dve.bn_stats(st1[:, t], x_mid[:, t]).then_inc(s["v_mv1"], 1)
                for i, t in enumerate(range(4 * half, 4 * half + 4)):
                    dve.wait_ge(s["v_mv1"], 8 * half + i + 1)
                    dve.bn_aggr(mv1[:, t], st1[:, t]).then_inc(s["v_mv1"], 1)

            def norms(half):
                dve.wait_ge(s["v_mv1"], 8 * (half + 1))
                dve.wait_ge(s["p_ln1"], 2 * half + 1)
                tiles = range(4 * half, 4 * half + 4)
                for t in tiles:
                    k.mark(dve.tensor_scalar(y0[:, t], x_mid[:, t], mv1[:, t, 0:1], r1[:, t:t + 1],
                                             ALU.subtract, ALU.mult))
                k.wait()
                dve.wait_ge(s["p_ln1"], 2 * half + 2)
                for t in tiles:
                    dve.tensor_scalar(nrow[:, t], y0[:, t], r1b[:, t:t + 1], None, ALU.mult
                                      ).then_inc(s["v_nrow"], 1)

            def mixed(half):
                h4 = slice(4 * half, 4 * half + 4)
                dve.wait_ge(s["t_z"], 4 * (half + 1))
                k.then(dve.tensor_tensor(z[:, h4], ps[:, 2 + half, :].rearrange("p (t e) -> p t e", e=E), y0[:, h4],
                                         ALU.add))
                for t in range(4 * half, 4 * half + 4):
                    dve.bn_stats(st2[:, t], z[:, t]).then_inc(s["v_mv2"], 1)
                for i, t in enumerate(range(4 * half, 4 * half + 4)):
                    dve.wait_ge(s["v_mv2"], 8 * half + i + 1)
                    dve.bn_aggr(mv2[:, t], st2[:, t]).then_inc(s["v_mv2"], 1)
                k.mark(dve.tensor_tensor(base[:, h4], z[:, h4], x_mid[:, h4], ALU.add))
                dve.wait_ge(s["v_mv2"], 8 * (half + 1))
                dve.wait_ge(s["p_ln2"], half + 1)
                for t in range(4 * half, 4 * half + 4):
                    dve.tensor_scalar(zn[:, t], z[:, t], mv2[:, t, 0:1], r2[:, t:t + 1],
                                      ALU.subtract, ALU.mult).then_inc(s["v_zn"], 1)

            def low_n2(half):
                cols = slice(512 * half, 512 * half + 512)
                dve.wait_ge(s["a_n2"], 2 * (half + 1))
                dve.tensor_tensor(n2_lo[:, cols], n2[:, cols], n2_hi[:, cols].bitcast(F32), ALU.subtract
                                  ).then_inc(s["v_n2lo"], 1)
            for half in range(2):
                heads(half)
                norms(half)
                mixed(half)
                low_n2(half)

            logits = ps[:, 6, 0:64].rearrange("p (t e) -> p t e", e=NX)
            wide = lambda n: rsm[:, n, :, None].to_broadcast([128, NT, NX])
            dve.wait_ge(s["t_router"], NT)
            dve.tensor_reduce(rsm[:, 0], logits, axis=AX.X, op=ALU.max).then_inc(s["v_rt"], 1)
            dve.wait_ge(s["v_rt"], 1)
            dve.tensor_tensor(rt[:, 0], logits, wide(0), ALU.subtract).then_inc(s["v_rt"], 1)
            dve.wait_ge(s["a_rexp"], 1)
            k.then(dve.tensor_reduce(rsm[:, 1], rt[:, 1], axis=AX.X, op=ALU.add))
            k.then(dve.reciprocal(rsm[:, 2], rsm[:, 1]))
            k.then(dve.tensor_tensor(rt[:, 2], rt[:, 1], wide(2), ALU.mult))
            rank_b = rank[:, None, :].to_broadcast([128, NT, NX])

            def first_largest(prob, mx, same, ranked, best, onehot):
                k.then(dve.tensor_reduce(rsm[:, mx], rt[:, prob], axis=AX.X, op=ALU.max))
                k.then(dve.tensor_tensor(rt[:, same], rt[:, prob], wide(mx), ALU.is_equal))
                k.then(dve.tensor_tensor(rt[:, ranked], rt[:, same], rank_b, ALU.mult))
                k.then(dve.tensor_reduce(rsm[:, best], rt[:, ranked], axis=AX.X, op=ALU.max))
                k.then(dve.tensor_tensor(rt[:, onehot], rt[:, ranked], wide(best), ALU.is_equal))

            first_largest(2, 3, 3, 4, 4, 5)
            k.then(dve.scalar_tensor_tensor(out=rt[:, 6], in0=rt[:, 5], scalar=-4.0, in1=rt[:, 2],
                                            op0=ALU.mult, op1=ALU.add))
            first_largest(6, 5, 7, 8, 6, 9)
            k.then(dve.tensor_tensor(rt[:, 10], rt[:, 5], rt[:, 9], ALU.add))
            dve.tensor_tensor(comb[:], rt[:, 10], rt[:, 2], ALU.mult).then_inc(s["v_comb"], 1)

            def h_low(g_base, g):
                n = g_base + g
                dve.wait_ge(s["a_hi"], n + 1)
                if not (isinstance(g_base, int) and n < 4):
                    dve.wait_ge(s["t_down"], n - 3)
                dve.tensor_tensor(h_lo[:, g % 4, :], h_f[:, g % 2, :], h_hi[:, g % 4, :].bitcast(F32),
                                  ALU.subtract).then_inc(s["v_lo"], 1)

            def combine(e, slot):
                bank = 6 - 2 * slot
                dve.wait_ge(s["t_down"], 4 * e + 4)
                dve.wait_ge(s["v_comb_e"], 2 * e + 1)
                dve.tensor_tensor(part, ps[:, bank:bank + 2, :].rearrange("p a n -> p (a n)"),
                                  comb_all[:, bass.ds(e, 1), :].squeeze(1), ALU.mult).then_inc(s["v_comb_e"], 1)
                dve.wait_ge(s["v_comb_e"], 2 * e + 2)
                dve.tensor_tensor(acc, part, acc, ALU.add).then_inc(s["v_comb_e"], 1)

            h_low(0, 0)
            h_low(0, 1)
            dve.memset(acc, 0.0).then_inc(s["v_comb_e"], 1)
            dve.wait_ge(s["t_b2"], NT)
            dve.tensor_tensor(base_b[:].rearrange("p t e -> p (t e)"), ps[:, 4:6, :].rearrange("p a n -> p (a n)"),
                              base[:].rearrange("p t e -> p (t e)"), ALU.add).then_inc(s["v_base"], 1)
            for g in range(2, 5):
                h_low(0, g)
            dve.wait_ge(s["comb_in"], 32)
            combine(0, 0)
            w_high(2, 0)
            for g in range(5, 8):
                h_low(0, g)
            with dve.Fori(1, NX // 2 - 1) as i:
                for u in range(2):
                    h_low(8 * i, 4 * u)
                    combine(2 * i + u - 1, 1 - u)
                    w_high(2 * i + u + 1, 1 - u)
                    for g in range(1, 4):
                        h_low(8 * i, 4 * u + g)
            last = NX - 2
            h_low(4 * last, 0)
            combine(last - 1, 1)
            w_high(last + 1, 1)
            for g in range(1, 5):
                h_low(4 * last, g)
            combine(last, 0)
            for g in range(5, 8):
                h_low(4 * last, g)
            combine(last + 1, 1)
            for half in range(2):
                dve.wait_ge(s["t_fin"], 4 * (half + 1))
                h4 = slice(4 * half, 4 * half + 4)
                dve.tensor_tensor(fin[:, h4], ps[:, half, :].rearrange("p (t e) -> p t e", e=E), base_b[:, h4],
                                  ALU.add).then_inc(s["v_fin"], 1)

        @blk.tensor
        def _(pe):
            pe.wait_ge(s["c_ident"], 1)
            pe.wait_ge(s["ld_ctx"], 48)
            for j in range(NT):
                pe.transpose(ps[:, 2 + j // 4, 128 * (j % 4):128 * (j % 4) + 128], cx[:, j], ident[:]
                             ).then_inc(s["t_ctx"], 1)
            for j in range(NT):
                pe.wait_ge(s["v_q"], j + 1)
                pe.transpose(ps[:, j // 4, 128 * (j % 4):128 * (j % 4) + 128], qn[:, j], ident[:]
                             ).then_inc(s["t_q"], 1)
            pe.wait_ge(s["a_k"], 8)
            pe.wait_ge(s["v_wc"], 1)
            pe.wait_ge(s["v_wq"], 3)
            for j in range(NT):
                pe.wait_ge(s["a_q"], j // 4 + 1)
                o = ps[:, 4, 16 * j:16 * j + 16]
                for g in range(2):
                    pe.matmul(o, k_m[:, j, g].rearrange("p b t -> p (b t)"), wc[:, g], start=(g == 0), stop=(g == 1))
                for b in range(2):
                    m = pe.matmul(o[64 * b:64 * b + 64], q_t[:, j, b], wq[:, b], start=False, stop=True,
                                  skip_group_check=True)
                m.then_inc(s["t_gates"], 1)
            pe.wait_ge(s["ld_vecs"], 80)
            pe.transpose(ps[:, 7, 256:292], vecs[:], ident[0:36, 0:36]).then_inc(s["t_vecs"], 1)

            def scores(n):
                j = ORDER[n]
                pe.wait_ge(s["v_qd"], 4 * (n + 1))
                if n >= 2:
                    pe.wait_ge(s["v_c"], n - 1)
                for g in range(2):
                    m = pe.matmul(ps[:, 2 + n % 2, 256 * g:256 * g + 256], k_m[:, j, g].rearrange("p b t -> p (b t)"),
                                  qd[:, n % 4, g].rearrange("p h s -> p (h s)"), start=True, stop=True)
                m.then_inc(s["t_qk"], 1)

            def log_decay(n):
                j = ORDER[n]
                o = ps[:, n % 2, :]
                if n >= 2:
                    pe.wait_ge(s["a_dec"], n - 1)
                pk = pick_r[:, j].rearrange("p b t -> p (b t)")
                wide_a = lambda t: t[:, NH * j:NH * j + NH, None].to_broadcast([128, NH, S])
                pe.matmul(o, pk, topx_hi[:].rearrange("p h s -> p (h s)"), start=True, stop=False)
                pe.matmul(o, pk, topx_lo[:].rearrange("p h s -> p (h s)"), start=False, stop=False)
                pe.matmul(o, ident_r[:], wide_a(a_hi), start=False, stop=False)
                pe.matmul(o, ident_r[:], wide_a(a_lo), start=False, stop=False)
                pe.matmul(o, ident_bf[:], later_bf[:, None, :].to_broadcast([128, NH, S]), start=False, stop=True
                          ).then_inc(s["t_l"], 1)

            def values(n):
                j = ORDER[n]
                jp, jh = j // 4, j % 4
                pe.wait_ge(s["v_c"], n + 1)
                for h in range(NH):
                    o = ps[64 * jp:64 * jp + 64, 4 + jh, 0:2 * NH * (DH + 1)].rearrange(
                        "p (b h d) -> p b h d", b=2, h=NH)[:, :, h, :]
                    m = pe.matmul(o, cmat[:, n % 2, h], v2[:, j, h], start=True, stop=True)
                m.then_inc(s["t_pv"], 1)

            pe.wait_ge(s["v_logf"], 1)
            pe.wait_ge(s["c_small"], 3)
            pe.matmul(ps[:, 5, 0:64], tri[:], logf[:].rearrange("p j h -> p (j h)"), start=True, stop=True
                      ).then_inc(s["t_cs"], 1)
            scores(0)
            pe.wait_ge(s["v_a"], 2)
            pe.matmul(ps[:, 6, 0:64], a_blk[:].rearrange("p b c -> p (b c)"), eye2[:], start=True, stop=True
                      ).then_inc(s["t_at"], 1)
            pe.wait_ge(s["a_cblk"], 2)
            pe.wait_ge(s["a_vecs"], 1)
            pe.matmul(ps[:, 7, 0:64], c_blk[:].rearrange("p b c -> p (b c)"), eye2[:], start=True, stop=True
                      ).then_inc(s["t_ct"], 1)
            scores(1)
            pe.wait_ge(s["v_topx"], 2)
            pe.wait_ge(s["v_ahl"], 4)
            pe.wait_ge(s["a_id"], 3)
            pe.wait_ge(s["c_masks"], 3)
            pe.wait_ge(s["a_v2"], 3)
            log_decay(0)
            pe.wait_ge(s["v_m"], 1)
            iv = ident[:].rearrange("p (b jp jh h) -> p jp b jh h", b=2, jh=4, jp=2)
            for jp in range(2):
                pe.matmul(ps[64 * jp:64 * jp + 64, 6, 128:192], m_full[:], iv[:, jp], start=True, stop=True
                          ).then_inc(s["t_em"], 1)
            log_decay(1)
            for j in range(NT):
                if j == 4:
                    pe.wait_ge(s["a_em"], 1)
                values(j)
                if j + 2 < NT:
                    scores(j + 2)
                    log_decay(j + 2)

            def token_tile(t):
                return slice(128 * (t % 4), 128 * (t % 4) + 128)

            for half in range(2):
                tiles = range(4 * half, 4 * half + 4)
                if half == 0:
                    pe.wait_ge(s["a_dec"], NT)
                for t in tiles:
                    pe.wait_ge(s["v_nrow"], t + 1)
                    pe.transpose(ps[:, half, token_tile(t)], nrow[:, t], ident[:]).then_inc(s["t_nrow"], 1)
                pe.wait_ge(s["a_nt"], half + 1)
                pe.wait_ge(s["ld_mix"], 32)
                pe.wait_ge(s["v_c"], NT)
                for t in tiles:
                    o = ps[:, 2 + half, token_tile(t)]
                    nt_tile = n_t[:, 128 * t:128 * t + 128]
                    pe.matmul(o, nt_tile, mixw[:], start=True, stop=False)
                    pe.matmul(o, nt_tile, ident[:], start=False, stop=False)
                    pe.matmul(o, ones_row[:], mixb[:], start=False, stop=True).then_inc(s["t_z"], 1)
                for t in tiles:
                    pe.wait_ge(s["v_zn"], t + 1)
                    pe.transpose(ps[:, half, token_tile(t)], zn[:, t], ident[:]).then_inc(s["t_n2"], 1)
            pe.wait_ge(s["ld_rw"], 32)
            pe.wait_ge(s["a_n2"], 4)
            pe.wait_ge(s["v_uc"], 2)
            for t in range(NT):
                pe.matmul(ps[:, 6, NX * t:NX * t + NX], n2[:, 128 * t:128 * t + 128], rw[:], start=True, stop=True
                          ).then_inc(s["t_router"], 1)

            def up(g_base, g):
                n = g_base + g
                slot, c = (g // FC) % 2, g % FC
                if g % FC == 0:
                    if isinstance(n, int):
                        e1 = n // FC + 1
                        pe.wait_ge(s["v_whi"], e1)
                        pe.wait_ge(s["p_wlo"], e1)
                if not (isinstance(n, int) and n < 2):
                    pe.wait_ge(s["a_hi"], n - 1)
                hi, lo = w_hi[:, slot, 128 * c:128 * c + 128], w_lo[:, slot, 128 * c:128 * c + 128]
                for half in range(2):
                    o = ps[:, 2 * (g % 2) + half, :]
                    cols = slice(512 * half, 512 * half + 512)
                    pe.matmul(o, hi, n2_hi[:, cols], start=True, stop=False)
                    pe.matmul(o, lo, n2_hi[:, cols], start=False, stop=False)
                    m = pe.matmul(o, hi, n2_lo[:, cols], start=False, stop=True)
                m.then_inc(s["t_up"], 1)

            def down(g_base, g):
                n = g_base + g
                slot, c = (g // FC) % 2, g % FC
                pe.wait_ge(s["v_lo"], n + 1)
                bank = 6 - 2 * slot
                hi = w_hi[:, slot, F + 128 * c:F + 128 * c + 128]
                lo = w_lo[:, slot, F + 128 * c:F + 128 * c + 128]
                for half in range(2):
                    o = ps[:, bank + half, :]
                    cols = slice(512 * half, 512 * half + 512)
                    pe.matmul(o, hi, h_hi[:, g % 4, cols], start=(c == 0), stop=False)
                    pe.matmul(o, lo, h_hi[:, g % 4, cols], start=False, stop=False)
                    m = pe.matmul(o, hi, h_lo[:, g % 4, cols], start=False, stop=(c == FC - 1))
                m.then_inc(s["t_down"], 1)

            pe.wait_ge(s["v_n2lo"], 2)
            up(0, 0)
            up(0, 1)
            pe.wait_ge(s["v_comb"], 1)
            for t in range(NT):
                pe.transpose(ps[0:NX, 4 + t // 4, token_tile(t)], comb[:, t], ident[:]).then_inc(s["t_combt"], 1)
            pe.wait_ge(s["a_combt"], 2)
            for t in range(NT):
                pe.matmul(ps[:, 4 + t // 4, token_tile(t)], comb_t[:, 128 * t:128 * t + 128], b2s[:],
                          start=True, stop=True).then_inc(s["t_b2"], 1)

            def turn(g_base, g):
                if isinstance(g_base, int) and g_base + g + 2 >= NX * FC:
                    pass
                else:
                    if (g + 2) % FC == 0 and not isinstance(g_base, int):
                        e1 = 2 * expert_pair + (g + 2) // FC + 1
                        pe.wait_ge(s["v_whi"], e1)
                        pe.wait_ge(s["p_wlo"], e1)
                    up(g_base, g + 2)
                if g == FC and isinstance(g_base, int) and g_base == 0:
                    pe.wait_ge(s["v_base"], 1)
                elif g % FC == 0 and not (isinstance(g_base, int) and g_base + g == 0):
                    if isinstance(g_base, int):
                        done = 2 * ((g_base + g) // FC - 2) + 2
                    else:
                        done = 4 * expert_pair + 2 * (g // FC) - 2
                    pe.wait_ge(s["v_comb_e"], done)
                down(g_base, g)

            for g in range(8):
                turn(0, g)
            with pe.Fori(1, NX // 2 - 1) as expert_pair:
                for g in range(8):
                    turn(8 * expert_pair, g)
            for g in range(8):
                turn(NX * FC - 8, g)
            pe.wait_ge(s["v_comb_e"], 2 * NX + 1)
            for t in range(NT):
                pe.transpose(ps[:, t // 4, token_tile(t)], acc[:, 128 * t:128 * t + 128], ident[:]
                             ).then_inc(s["t_fin"], 1)


INPUTS = ["x", "ctx_1024", "L0_xattn_igate_kernel", "L0_xattn_igate_bias", "L0_xattn_fgate_kernel",
          "L0_xattn_fgate_bias", "L0_xattn_outnorm_weight", "L0_ffn_g1", "L0_ffn_be1", "L0_ffn_mix_w",
          "L0_ffn_mix_b", "L0_ffn_g2", "L0_ffn_be2", "L0_ffn_router_w", "L0_ffn_w1", "L0_ffn_b1",
          "L0_ffn_w2", "L0_ffn_b2"]


def kernel(**inputs):
    import numpy as np
    import concourse.bacc as bacc
    from concourse.bass_utils import run_bass_kernel_spmd

    nc = bacc.Bacc("TRN2", target_bir_lowering=False, num_devices=1)
    arrays, args = {}, []
    for name in INPUTS:
        a = np.ascontiguousarray(inputs[name])
        arrays[f"in_{name}"] = a
        args.append(nc.dram_tensor(f"in_{name}", a.shape, mybir.dt.from_np(a.dtype), kind="ExternalInput").ap())
    out = nc.dram_tensor("out", (B, S, E), F32, kind="ExternalOutput").ap()
    build(nc, *args, out)
    r = run_bass_kernel_spmd(nc, [arrays], core_ids=[0])
    return r.results[0]["out"]
```

```python
from contextlib import ExitStack

import concourse.bass as bass
from concourse import mybir

ALU = mybir.AluOpType
ACT = mybir.ActivationFunctionType
AX = mybir.AxisListType
F32 = mybir.dt.float32
F32R = mybir.dt.float32r
BF16 = mybir.dt.bfloat16

B, S, E, NH = 16, 64, 128, 8
DH = E // NH
TOK = B * S
NT = TOK // 128
NX, F = 8, 512
FC = F // 128
B1_AT, G1_AT, G2_AT, B2_AT, NVEC = 0, NX * FC, NX * FC + 2, NX * FC + 4, NX * FC + 4 + NX
NEG = -1.0e30
LOWEST = -3.0e38
ORDER = [jp * (NT // 2) + jh for jh in range(NT // 2) for jp in range(2)]
UW = DH + 2
SCORE_BANK = (2, 3, 6, 7, 2, 3, 2, 3)
BY_POOL = (0, 1, 2, 3, 7)
QN_BY_ACT = 5
T_BANK, Z_BANK = (4, 7), (5, 5, 2, 3)
EARLY, LAST = 2, NX * FC - 1
RS_WRITTEN = [0, 1, 2, 4, 5, 7, 8, 9]
FILL_START, FILL_SUMS, FILL_HEADS, FILL_NORMS, FILL_Z, FILL_ROUTE, FILL_UP = 11, 1, 19, 1, 1, 4, 3


class Steps:

    def __init__(self, engine, sem):
        self.engine, self.sem, self.n = engine, sem, 0

    def mark(self, instruction):
        instruction.then_inc(self.sem, 1)
        self.n += 1

    def wait(self):
        self.engine.wait_ge(self.sem, self.n)

    def then(self, instruction):
        self.mark(instruction)
        self.wait()


def build(nc, x, ctx_in, ig_k, ig_b, fg_k, fg_b, onorm_w, g1, be1, mix_w, mix_b, g2, be2,
          router_w, w1, b1, w2, b2, out):
    stack = ExitStack()
    with stack:
        def sb(name, shape, dt=F32):
            return stack.enter_context(nc.sbuf_tensor(name, shape, dt))

        def sem(name):
            return stack.enter_context(nc.semaphore(name))

        ident = sb("ident", [128, 128])
        ident_r = sb("ident_r", [128, 128], F32R)
        ident_bf = sb("ident_bf", [128, 128], BF16)
        eye2 = sb("eye2", [128, S])
        tri = sb("tri", [128, 128])
        later_bf = sb("later_bf", [128, S], BF16)
        pick = sb("pick", [128, NT, 2, S])
        pick_r = sb("pick_r", [128, NT, 2, S], F32R)
        head_of_row = sb("head_of_row", [128, NH, 16])
        h8 = sb("h8", [128, NH])
        e8 = sb("e8", [128, NH])
        e4 = sb("e4", [128, NH // 2])
        zeros = sb("zeros", [128, S])
        rank = sb("rank", [128, NX])
        ones_row = sb("ones_row", [1, 128])
        comb_all = sb("comb_all", [128, NX, TOK])
        x1 = comb_all[:, 0].rearrange("p (j e) -> p j e", e=E)
        cx = comb_all[:, 1].rearrange("p (j e) -> p j e", e=E)
        qn = comb_all[:, 2].rearrange("p (j e) -> p j e", e=E)
        q_t = comb_all[:, 3].rearrange("p (j b t) -> p j b t", b=2, t=S)
        k_m = comb_all[:, 4:6].rearrange("p a (j g b t) -> p (a j) g b t", g=2, b=2, t=S)
        qd = comb_all[:, 6:8].rearrange("p a (r g h s) -> p (a r) g h s", r=2, g=2, s=S)
        x2 = sb("x2", [128, NT, E])
        wg = sb("wg", [128, 3, 2, 16])
        wq = sb("wq", [128, 2, 16])
        wc = sb("wc", [128, 2, 16])
        gbias = sb("gbias", [128, 16])
        onw = sb("onw", [128, E])
        vecs = sb("vecs", [NVEC, 128])
        vecs_t = sb("vecs_t", [128, NVEC])
        mixw = sb("mixw", [128, E])
        mixb = sb("mixb", [1, E])
        rw = sb("rw", [128, NX])
        stats = sb("stats", [128, NT, 6])
        mv = sb("mv", [128, NT, 2])
        rstd = sb("rstd", [128, NT])
        mr0 = sb("mr0", [128, NT])
        vsum = sb("vsum", [128, NT, NH])
        v2 = sb("v2", [128, NT, NH, 2, UW])
        gates = sb("gates", [128, NT, 16])
        absf = sb("absf", [128, NT, NH])
        ef = sb("ef", [128, NT, NH])
        lnf = sb("lnf", [128, NT, NH])
        logf = sb("logf", [128, NT, NH])
        a_hi = sb("a_hi", [128, NT * NH], F32R)
        a_lo = sb("a_lo", [128, NT * NH], F32R)
        a_blk = sb("a_blk", [128, 2, NT * NH])
        c_blk = sb("c_blk", [128, 2, NT * NH])
        top_a = sb("top_a", [128, S])
        top_hi = sb("top_hi", [128, S], F32R)
        top_lo = sb("top_lo", [128, S], F32R)
        m_full = sb("m_full", [128, S])
        topx_hi = sb("topx_hi", [128, NH, S], F32R)
        topx_lo = sb("topx_lo", [128, NH, S], F32R)
        em = sb("em", [128, 4, 2, NH])
        dec = sb("dec", [128, 2, NH * S])
        cmat = sb("cmat", [128, 2, NH, S])
        rs_in = sb("rs_in", [128, 7, 32])
        rs_ln = sb("rs_ln", [128, 7, 32])
        rs_0 = sb("rs_0", [128, 7, 32])
        rs_h = sb("rs_h", [128, 7, 32])
        rs_t = sb("rs_t", [128, 7, 32])
        rs_q = sb("rs_q", [128, 7, 32])
        t1 = sb("t1", [128, 2, 32])
        nrm = sb("nrm", [128, 2, 32])
        rn = sb("rn", [128, 2, 32])
        uc = sb("uc", [128, 2, 4 * E])
        usq = sb("usq", [128, 2, 4 * E])
        v16 = sb("v16", [128, 2, 32])
        rn2 = sb("rn2", [128, 2, 32])
        hv = sb("hv", [128, 2, 32])
        hf = sb("hf", [128, 2, 32])
        hmean = sb("hmean", [128, 2, 32])
        h_f = sb("h_f", [128, 2, TOK])
        ucw = h_f[:, 0].rearrange("p (t e) -> p t e", e=E)
        att = h_f[:, 1].rearrange("p (t e) -> p t e", e=E)
        x_mid = sb("x_mid", [128, NT, E])
        st1 = sb("st1", [128, NT, 6])
        mv1 = sb("mv1", [128, NT, 2])
        r1 = sb("r1", [128, 2, 2, 4])
        mr1 = sb("mr1", [128, 2, 2, 4])
        mr2 = sb("mr2", [128, NT])
        y0 = sb("y0", [128, NT, E])
        nrow = sb("nrow", [128, NT, E])
        n_t = sb("n_t", [128, TOK])
        c_t = sb("c_t", [128, NT, 2, S])
        zn = c_t[:].rearrange("p j b t -> p j (b t)")
        st2 = sb("st2", [128, NT, 6])
        mv2 = sb("mv2", [128, NT, 2])
        r2 = sb("r2", [128, NT])
        base = sb("base", [128, NT, E])
        n2 = sb("n2", [128, TOK])
        n2_hi = sb("n2_hi", [128, TOK], F32R)
        n2_lo = sb("n2_lo", [128, TOK], F32R)
        rsm = sb("rsm", [128, 8, NT])
        rt = sb("rt", [128, 12, NT, NX])
        comb = sb("comb", [128, NT, NX])
        comb_t = sb("comb_t", [NX, TOK])
        raw = sb("raw", [128, 2, 2 * F])
        part = uc[:].rearrange("p a n -> p (a n)")
        acc = usq[:].rearrange("p a n -> p (a n)")
        fin = y0
        w_hi = sb("w_hi", [128, 2, 2 * F], F32R)
        w_lo = sb("w_lo", [128, 2, 2 * F], F32R)
        b1_now = sb("b1_now", [128, 2, FC])
        h_hi = sb("h_hi", [128, 4, TOK], F32R)
        h_lo = sb("h_lo", [128, 4, TOK], F32R)
        comb_dram = nc.dram_tensor("comb_dram", (NX, TOK), F32, kind="Internal").ap()

        ps = stack.enter_context(nc.psum_tensor("ps", [128, 8, 512], F32))

        names = (
            "ld_x ld_ctx ld_gate ld_x2 ld_onw ld_vecs ld_mix ld_rw ld_raw0 ld_raw1 "
            "c_pool c_ident c_pick c_masks c_v2zero c_small c_blkzero c_kzero "
            "p_ucw p_xmid p_y0 p_qd p_wlo "
            "v_first v_att v_wq v_stats v_rs v_vsum v_newton v_mr0 v_mr1 v_q v_logf v_chain v_gates v_absf v_a "
            "v_ahl v_scan v_topx v_m v_qd v_c v_small v_h8 v_wc v_mixw v_uc v_mv1 v_base v_mr2 v_nrow v_mv2 "
            "v_zn v_n2lo v_rt v_comb v_lo v_comb_e v_whi v_b1 v_fin v_combt "
            "a_first a_k a_q a_v2 a_exp a_ln a_cblk a_em a_dec a_usq a_rs a_qn a_nrow a_zn a_nt a_n2 a_rexp a_hi "
            "a_vecs a_id a_ct "
            "t_first t_ctx t_q t_gates t_cs t_at t_ct t_em t_vecs t_l t_qk t_pv t_nrow t_z t_n2 t_router "
            "t_combt t_up t_down t_acc t_fin "
            "comb_out comb_first comb_rest out_done"
        ).split()
        s = {n: sem(n) for n in names}
        ld_raw = [s["ld_raw0"], s["ld_raw1"]]

        def u_half(half):
            v = ps[:, 4 + 2 * half:6 + 2 * half, 0:2 * NH * UW]
            return v.rearrange("p j (c d) -> p j c d", d=UW)

        blk = stack.enter_context(nc.Block())
        xv = x.rearrange("(j b) s (g e) -> b s j g e", b=2, g=2)
        cv = ctx_in.rearrange("(j b) s (g e) -> b s j g e", b=2, g=2)
        x1v = x1.rearrange("p j (g e) -> p j g e", g=2)
        cxv = cx.rearrange("p j (g e) -> p j g e", g=2)
        x2v = x.rearrange("(jp t) s e -> jp s t e", jp=2)
        outv = out.rearrange("(jp t) s e -> jp s t e", jp=2)

        def load_raw(eng, e, slot):
            if isinstance(e, int):
                a, b = w1[e], w2[e]
            else:
                a, b = w1[bass.ds(e, 1), :, :].squeeze(0), w2[bass.ds(e, 1), :, :].squeeze(0)
            eng.dma_start(raw[:, slot, 0:F], a).then_inc(ld_raw[slot], 16)
            eng.dma_start(raw[:, slot, F:2 * F].rearrange("p (c d) -> p c d", c=FC),
                          b.rearrange("(c p) d -> p c d", p=128)).then_inc(ld_raw[slot], 16)

        def spread_before(n):
            return sum((m in BY_POOL) == (n in BY_POOL) for m in range(n))

        def q_diag(engine, n, done, own_wait=False):
            j = ORDER[n]
            engine.wait_ge(s["a_q"], j // 4 + 1)
            engine.wait_ge(s["c_small"], 3)
            if n >= 4:
                engine.wait_ge(s["t_qk"], n - 3)
            for rh in range(2):
                rows = slice(64 * rh, 64 * rh + 64)
                for g in range(2):
                    engine.tensor_tensor(qd[rows, n % 4, g], q_t[rows, j, rh ^ g, None, :].to_broadcast([64, 4, S]),
                                         e4[rows, :, None].to_broadcast([64, 4, S]), ALU.mult).then_inc(done, 1)
                if own_wait:
                    engine.wait_ge(done, 4 * spread_before(n) + 2 * (rh + 1))

        @blk.sync
        def _(sp):
            sp.dma_start(x1v[0:64], xv[0]).then_inc(s["ld_x"], 16)
            for g in range(2):
                sp.dma_start(x1v[64:128, :, 1 - g], xv[1, :, :, g]).then_inc(s["ld_x"], 16)
            sp.dma_start(cxv[0:64], cv[0]).then_inc(s["ld_ctx"], 16)
            for g in range(2):
                sp.dma_start(cxv[64:128, :, 1 - g], cv[1, :, :, g]).then_inc(s["ld_ctx"], 16)
            for half in range(2):
                for n, kern in ((0, fg_k), (1, ig_k)):
                    sp.dma_start(wg[64 * half:64 * half + 64, :, :, 8 * n:8 * n + 8],
                                 kern.rearrange("(c g r) h -> r c g h", c=3, g=2)).then_inc(s["ld_gate"], 16)
            for n, bias in ((0, fg_b), (1, ig_b)):
                sp.dma_start(gbias[:, 8 * n:8 * n + 8],
                             bias.rearrange("(a h) -> a h", a=1).to_broadcast([128, NH])).then_inc(s["ld_gate"], 16)
            for jp in range(2):
                sp.dma_start(x2[64 * jp:64 * jp + 64], x2v[jp]).then_inc(s["ld_x2"], 16)
            load_raw(sp, 0, 0)
            sp.dma_start(vecs[B1_AT:G1_AT, :], b1.rearrange("e (c f) -> (e c) f", f=128)).then_inc(s["ld_vecs"], 16)
            for n, v in enumerate((g1, be1, g2, be2)):
                sp.dma_start(vecs[G1_AT + n:G1_AT + n + 1, :],
                             v.rearrange("(a n) -> a n", a=1)).then_inc(s["ld_vecs"], 16)
            sp.dma_start(vecs[B2_AT:NVEC, :], b2).then_inc(s["ld_vecs"], 16)
            sp.dma_start(onw[:], onorm_w.rearrange("h d -> (h d)").rearrange("(a n) -> a n", a=1)
                         .to_broadcast([128, E])).then_inc(s["ld_onw"], 16)
            sp.dma_start(mixw[:], mix_w).then_inc(s["ld_mix"], 16)
            sp.dma_start(mixb[:], mix_b.rearrange("(a n) -> a n", a=1)).then_inc(s["ld_mix"], 16)
            sp.dma_start(rw[:], router_w).then_inc(s["ld_rw"], 16)
            load_raw(sp, 1, 1)

            def load_next(e, slot):
                sp.wait_ge(s["v_whi"], e - 1)
                sp.wait_ge(s["p_wlo"], e - 1)
                load_raw(sp, e, slot)

            load_next(2, 0)
            load_next(3, 1)
            sp.wait_ge(s["v_combt"], 2)
            sp.dma_start(comb_dram, comb_t[:]).then_inc(s["comb_out"], 16)
            sp.wait_ge(s["comb_out"], 16)
            for done, e0, n in ((s["comb_first"], 0, 2), (s["comb_rest"], 2, NX - 2)):
                sp.dma_start(comb_all[:, e0:e0 + n, :],
                             comb_dram[e0:e0 + n, :].rearrange("(a e) t -> a e t", a=1)
                             .to_broadcast([128, n, TOK])).then_inc(done, 16)
            with sp.Fori(2, NX // 2) as i:
                for slot in range(2):
                    load_next(2 * i + slot, slot)
            for half in range(2):
                h4 = slice(4 * half, 4 * half + 4)
                sp.wait_ge(s["v_fin"], half + 1)
                for jp in range(2):
                    sp.dma_start(outv[jp, :, h4], fin[64 * jp:64 * jp + 64, h4]).then_inc(s["out_done"], 16)
            sp.wait_ge(s["out_done"], 64)

        @blk.gpsimd
        def _(pool):
            k = Steps(pool, s["c_pool"])
            k.then(pool.memset(ident[:], 0.0))
            pool.affine_select(out=ident[:], in_=ident[:], compare_op=ALU.not_equal, fill=1.0, base=0,
                               pattern=[[-1, 128]], channel_multiplier=1).then_inc(s["c_ident"], 1)
            for t in (tri, pick, e8, head_of_row):
                k.mark(pool.memset(t[:], 1.0))
            k.mark(pool.memset(later_bf[:], 0.0))
            k.wait()
            pool.wait_ge(s["c_ident"], 1)
            pool.tensor_tensor(eye2[:], ident[:, 0:S], ident[:, S:128], ALU.add).then_inc(s["c_small"], 1)
            k.then(pool.affine_select(out=tri[:], in_=tri[:], compare_op=ALU.is_ge, fill=0.0, base=0,
                                      pattern=[[1, 128]], channel_multiplier=-1))
            pool.memset(tri[0:64, 64:128], 0.0).then_inc(s["c_small"], 1)
            pool.wait_ge(s["c_small"], 2)
            k.then(pool.affine_select(out=e8[:], in_=e8[:], compare_op=ALU.is_ge, fill=0.0, base=0,
                                      pattern=[[-DH, NH]], channel_multiplier=1))
            k.then(pool.affine_select(out=e8[:], in_=e8[:], compare_op=ALU.is_ge, fill=0.0, base=DH - 1,
                                      pattern=[[DH, NH]], channel_multiplier=-1))
            k.then(pool.tensor_scalar(e8[:], e8[:], DH ** -0.5, None, ALU.mult))
            pool.tensor_tensor(e4[:], e8[:, 0:4], e8[:, 4:8], ALU.add).then_inc(s["c_small"], 1)
            pool.affine_select(out=head_of_row[:], in_=head_of_row[:], compare_op=ALU.is_equal, fill=0.0, base=0,
                               pattern=[[-1, NH], [-NH, 16]], channel_multiplier=1).then_inc(s["c_masks"], 1)
            pool.wait_ge(s["c_masks"], 1)
            for b in range(2):
                pool.affine_select(out=later_bf[64 * b:64 * b + 64], in_=later_bf[64 * b:64 * b + 64],
                                   compare_op=ALU.is_ge, fill=NEG, base=0,
                                   pattern=[[1, S]], channel_multiplier=-1).then_inc(s["c_masks"], 1)
                pool.wait_ge(s["c_masks"], b + 2)
            v = pick[:]
            k.then(pool.affine_select(out=v, in_=v, compare_op=ALU.is_ge, fill=0.0, base=0,
                                      pattern=[[-NH, NT], [-64, 2], [0, S]], channel_multiplier=1))
            pool.affine_select(out=v, in_=v, compare_op=ALU.is_ge, fill=0.0, base=NH - 1,
                               pattern=[[NH, NT], [64, 2], [0, S]], channel_multiplier=-1).then_inc(s["c_pick"], 1)
            pool.memset(v2[:], 0.0).then_inc(s["c_v2zero"], 1)
            pool.wait_ge(s["c_v2zero"], 1)
            for b in range(2):
                pool.memset(v2[64 * b:64 * b + 64, :, :, b, DH:DH + 1], 1.0).then_inc(s["c_v2zero"], 1)
                pool.wait_ge(s["c_v2zero"], b + 2)

            def weigh_heads(half):
                pool.wait_ge(s["v_uc"], half + 1)
                pool.tensor_tensor(ucw[:, 4 * half:4 * half + 4], uc[:, half].rearrange("p (t e) -> p t e", e=E),
                                   onw[:, None, :].to_broadcast([128, 4, E]), ALU.mult).then_inc(s["p_ucw"], 1)

            def first_norm(half):
                pool.wait_ge(s["v_mr1"], half + 1)
                for i in range(4):
                    pool.tensor_scalar(y0[:, 4 * half + i], x_mid[:, 4 * half + i], r1[:, half, 0, i:i + 1],
                                       mr1[:, half, 0, i:i + 1], ALU.mult, ALU.add).then_inc(s["p_y0"], 1)

            def w_low(e, slot):
                pool.wait_ge(s["v_whi"], e + 1)
                pool.tensor_tensor(w_lo[:, slot, :], raw[:, slot, :], w_hi[:, slot, :].bitcast(F32), ALU.subtract
                                   ).then_inc(s["p_wlo"], 1)

            q_diag(pool, 0, s["p_qd"], own_wait=True)
            q_diag(pool, 1, s["p_qd"], own_wait=True)
            q_diag(pool, 2, s["p_qd"], own_wait=True)
            q_diag(pool, 3, s["p_qd"], own_wait=True)
            w_low(0, 0)
            q_diag(pool, 7, s["p_qd"], own_wait=True)
            pool.wait_ge(s["ld_onw"], 16)
            weigh_heads(0)
            w_low(1, 1)
            pool.wait_ge(s["ld_x2"], 32)
            pool.wait_ge(s["v_att"], 1)
            pool.tensor_tensor(x_mid[:, 0:4], att[:, 0:4], x2[:, 0:4], ALU.add).then_inc(s["p_xmid"], 1)
            weigh_heads(1)
            first_norm(0)
            first_norm(1)
            with pool.Fori(1, NX // 2) as i:
                for slot in range(2):
                    w_low(2 * i + slot, slot)

        def z_tile(t):
            at = 128 * (t % 4 if t < 4 else t % 2)
            return ps[:, Z_BANK[t // 2], at:at + 128]

        def up_bank(g):
            return 2 * ((g + 1) % 2)

        @blk.scalar
        def _(act):
            act.preload_act_table_set("natural_log_exp_and_others")
            act.wait_ge(s["c_ident"], 1)
            act.activation(ident_r[:], ident[:], ACT.Copy).then_inc(s["a_id"], 1)
            act.activation(ident_bf[:], ident[:], ACT.Copy).then_inc(s["a_id"], 1)

            def rsqrt_guess(u, k, n):
                act.wait_ge(s["v_rs"], RS_WRITTEN[k])
                act.activation(rs_ln[:, u, 0:n], rs_in[:, u, 0:n], ACT.Ln).then_inc(s["a_rs"], 1)
                act.wait_ge(s["a_rs"], 2 * k - 1)
                act.activation(rs_0[:, u, 0:n], rs_ln[:, u, 0:n], ACT.Exp, scale=-0.5).then_inc(s["a_rs"], 1)

            rsqrt_guess(0, 1, NT)
            for a in range(2):
                act.wait_ge(s["t_ctx"], 4 * (a + 1))
                act.activation(c_t[:, 4 * a:4 * a + 4].rearrange("p j b t -> p (j b t)"), ps[:, 2 + a, :],
                               ACT.Copy).then_inc(s["a_ct"], 1)
            act.wait_ge(s["v_mr0"], 1)
            for j in range(QN_BY_ACT, NT):
                act.activation(qn[:, j], x1[:, j], ACT.Identity, bias=mr0[:, j:j + 1], scale=rstd[:, j:j + 1]
                               ).then_inc(s["a_qn"], 1)
            for a in range(2):
                act.wait_ge(s["t_q"], 4 * (a + 1))
                act.activation(q_t[:, 4 * a:4 * a + 4].rearrange("p j b t -> p (j b t)"), ps[:, a, :],
                               ACT.Copy).then_inc(s["a_q"], 1)
            act.wait_ge(s["c_kzero"], 1)
            kv = k_m.rearrange("p (a j) g b t -> p a j g b t", a=2)
            pv = ps[:, 2:4, :].rearrange("p a (j b t) -> p a j b t", j=4, b=2)

            def keys(a):
                for rh in range(2):
                    for b in range(2):
                        act.activation(kv[64 * rh:64 * rh + 64, a, :, rh ^ b, b, :],
                                       pv[64 * rh:64 * rh + 64, a, :, b, :], ACT.Copy).then_inc(s["a_k"], 1)

            keys(0)
            act.wait_ge(s["v_absf"], 1)
            act.activation(ef[:], absf[:], ACT.Exp, scale=-1.0).then_inc(s["a_exp"], 1)
            act.wait_ge(s["a_exp"], 1)
            act.activation(lnf[:], ef[:], ACT.Ln, bias=1.0).then_inc(s["a_ln"], 1)
            keys(1)
            act.wait_ge(s["t_cs"], 1)
            act.wait_ge(s["v_a"], 2)
            act.wait_ge(s["c_blkzero"], 2)
            for b in range(2):
                act.activation(c_blk[64 * b:64 * b + 64, b, :], ps[64 * b:64 * b + 64, 5, 0:64],
                               ACT.Copy).then_inc(s["a_cblk"], 1)
            act.wait_ge(s["t_vecs"], 1)
            act.activation(vecs_t[:], ps[:, 1, 256:256 + NVEC], ACT.Copy).then_inc(s["a_vecs"], 1)
            act.wait_ge(s["c_pick"], 1)
            act.activation(pick_r[:], pick[:], ACT.Copy).then_inc(s["a_id"], 1)
            act.wait_ge(s["c_v2zero"], 3)
            cb = cx.rearrange("p j (g h d) -> p j g h d", g=2, h=4)
            act.activation(v2[0:64, :, :, 0, 0:DH], cx[0:64].rearrange("p j (h d) -> p j h d", h=NH),
                           ACT.Copy).then_inc(s["a_v2"], 1)
            for g in range(2):
                act.activation(v2[64:128, :, 4 * g:4 * g + 4, 1, 0:DH], cb[64:128, :, 1 - g],
                               ACT.Copy).then_inc(s["a_v2"], 1)

            def decay(j):
                act.wait_ge(s["t_l"], j + 1)
                if j >= 2:
                    act.wait_ge(s["v_c"], j - 1)
                act.activation(dec[:, j % 2, :], ps[:, j % 2, :], ACT.Exp).then_inc(s["a_dec"], 1)

            def centred_squares(half):
                act.wait_ge(s["v_uc"], half + 1)
                act.activation(usq[:, half, :], uc[:, half, :], ACT.Square).then_inc(s["a_usq"], 1)

            def centre(out, src, bias, scale, n, sem_a):
                for i in range(n):
                    act.activation(out[:, i], src[i], ACT.Identity, bias=bias[:, i:i + 1],
                                   scale=scale[:, i:i + 1]).then_inc(sem_a, 1)

            def affine_t(half, out, col, sem_t, sem_a):
                act.wait_ge(sem_t, 4 * (half + 1))
                act.activation(out[:, 512 * half:512 * half + 512], ps[:, T_BANK[half], :], ACT.Identity,
                               bias=vecs_t[:, col + 1:col + 2], scale=vecs_t[:, col:col + 1]).then_inc(sem_a, 1)

            for n in range(NT):
                if n == 6:
                    rsqrt_guess(1, 2, 32)
                decay(n)
                if n == 0:
                    act.wait_ge(s["t_em"], 2)
                    act.activation(em[:].rearrange("p jh b h -> p b jh h"),
                                   ps[:, 5, 64:128].rearrange("p (b jh h) -> p b jh h", b=2, h=NH),
                                   ACT.Exp, scale=-1.0).then_inc(s["a_em"], 1)
                if n == 5:
                    centred_squares(0)
            rsqrt_guess(3, 3, 8)
            centred_squares(1)
            rsqrt_guess(2, 4, 32)
            act.wait_ge(s["v_mr1"], 1)
            centre(nrow, [x_mid[:, t] for t in range(4)], mr1[:, 0, 1], r1[:, 0, 1], 4, s["a_nrow"])
            affine_t(0, n_t, G1_AT, s["t_nrow"], s["a_nt"])
            rsqrt_guess(4, 5, 8)
            act.wait_ge(s["v_mr1"], 2)
            centre(nrow[:, 4:8], [x_mid[:, t] for t in (4, 5)], mr1[:, 1, 1], r1[:, 1, 1], 2, s["a_nrow"])
            affine_t(1, n_t, G1_AT, s["t_nrow"], s["a_nt"])
            rsqrt_guess(5, 6, 4)
            act.wait_ge(s["v_mr2"], 1)
            centre(zn, [z_tile(t) for t in range(4)], mr2, r2, 4, s["a_zn"])
            rsqrt_guess(6, 7, 4)
            affine_t(0, n2, G2_AT, s["t_n2"], s["a_n2"])
            act.wait_ge(s["v_mr2"], 2)
            centre(zn[:, 4:8], [z_tile(t) for t in (4, 5)], mr2[:, 4:8], r2[:, 4:8], 2, s["a_zn"])
            affine_t(0, n2_hi, G2_AT, s["t_n2"], s["a_n2"])
            affine_t(1, n2, G2_AT, s["t_n2"], s["a_n2"])
            affine_t(1, n2_hi, G2_AT, s["t_n2"], s["a_n2"])
            act.wait_ge(s["v_rt"], 2)
            act.activation(rt[:, 1], rt[:, 0], ACT.Exp).then_inc(s["a_rexp"], 1)
            act.preload_act_table_set("silu_and_others")

            def hidden(i, g):
                n, expert = 8 * i + g, 2 * i + g // FC
                first = isinstance(i, int)
                act.wait_ge(s["t_up"], n + 1)
                bank = 2 * g if first and n < EARLY else 4 if first and n == EARLY else up_bank(g)
                src = ps[:, bank:bank + 2, :].rearrange("p a n -> p (a n)")
                bias = b1_now[:, g // FC % 2, g % FC:g % FC + 1]
                if g % FC == 0:
                    act.wait_ge(s["v_b1"], expert + 1)
                if not (first and n < 2):
                    act.wait_ge(s["v_lo"], n - 1)
                act.activation(h_f[:, g % 2, :], src, ACT.Silu, bias=bias)
                if not (first and n < 4):
                    act.wait_ge(s["t_down"], n - 3)
                act.activation(h_hi[:, g % 4, :], src, ACT.Silu, bias=bias).then_inc(s["a_hi"], 1)

            act.wait_ge(s["v_b1"], 1)
            for half, sem_up, sem_hi in ((0, s["t_first"], s["a_first"]), (1, s["t_up"], s["a_hi"])):
                cols = slice(512 * half, 512 * half + 512)
                act.wait_ge(sem_up, 1)
                act.activation(h_f[:, 0, cols], ps[:, half, :], ACT.Silu, bias=b1_now[:, 0, 0:1])
                act.activation(h_hi[:, 0, cols], ps[:, half, :], ACT.Silu, bias=b1_now[:, 0, 0:1]
                               ).then_inc(sem_hi, 1)
            for g in range(1, 8):
                hidden(0, g)
            with act.Fori(1, NX // 2 - 1) as i:
                for g in range(8):
                    hidden(i, g)
            for g in range(7):
                hidden(NX // 2 - 1, g)
            act.wait_ge(s["v_lo"], LAST - 1)
            act.wait_ge(s["t_down"], LAST - 3)
            for half in range(2):
                cols = slice(512 * half, 512 * half + 512)
                src, bias = ps[:, up_bank(LAST) + half, :], b1_now[:, 1, FC - 1:FC]
                act.wait_ge(s["t_up"], LAST + 1 + half)
                act.activation(h_f[:, 1, cols], src, ACT.Silu, bias=bias)
                act.activation(h_hi[:, 3, cols], src, ACT.Silu, bias=bias).then_inc(s["a_hi"], 1)

        @blk.vector
        def _(dve):
            k = Steps(dve, s["v_chain"])
            dve.memset(zeros[:], 0.0).then_inc(s["v_small"], 1)
            for e in range(NX):
                m = dve.memset(rank[:, e:e + 1], float(NX - e))
            m.then_inc(s["v_small"], 1)
            dve.memset(ones_row[:], 1.0).then_inc(s["v_small"], 1)
            dve.memset(k_m, 0.0).then_inc(s["c_kzero"], 1)
            dve.memset(a_blk[:], 0.0).then_inc(s["c_blkzero"], 1)
            dve.memset(c_blk[:], 0.0).then_inc(s["c_blkzero"], 1)
            dve.wait_ge(s["ld_x"], 48)
            for j in range(NT):
                dve.bn_stats(stats[:, j], x1[:, j]).then_inc(s["v_stats"], 1)
            for j in range(NT):
                dve.wait_ge(s["v_stats"], j + 1)
                dve.bn_aggr(mv[:, j], stats[:, j]).then_inc(s["v_stats"], 1)

            def rsqrt_begin(u, n):
                k.mark(dve.tensor_scalar(rs_h[:, u, 0:n], rs_in[:, u, 0:n], -0.5, None, ALU.mult))

            def rsqrt_end(u, n, guess, dst, times=None):
                dve.wait_ge(s["a_rs"], 2 * guess)
                r0 = rs_0[:, u, 0:n]
                k.mark(dve.tensor_tensor(rs_t[:, u, 0:n], r0, r0, ALU.mult))
                if times is not None:
                    k.mark(dve.tensor_tensor(rs_q[:, u, 0:n], r0, times, ALU.mult))
                    r0 = rs_q[:, u, 0:n]
                k.wait()
                k.then(dve.tensor_tensor(rs_h[:, u, 0:n], rs_t[:, u, 0:n], rs_h[:, u, 0:n], ALU.mult))
                dve.scalar_tensor_tensor(out=dst, in0=rs_h[:, u, 0:n], scalar=1.5, in1=r0, op0=ALU.add,
                                         op1=ALU.mult).then_inc(s["v_newton"], 1)

            dve.wait_ge(s["v_stats"], 2 * NT)
            dve.tensor_scalar(rs_in[:, 0, 0:NT], mv[:, :, 1], 1e-5, None, ALU.add).then_inc(s["v_rs"], 1)
            dve.wait_ge(s["v_rs"], 1)
            rsqrt_begin(0, NT)
            rsqrt_end(0, NT, 1, rstd[:])
            dve.wait_ge(s["v_newton"], 1)
            dve.scalar_tensor_tensor(out=mr0[:], in0=mv[:, :, 0], scalar=-1.0, in1=rstd[:], op0=ALU.mult,
                                     op1=ALU.mult).then_inc(s["v_mr0"], 1)
            for j in range(QN_BY_ACT):
                dve.tensor_scalar(qn[:, j], x1[:, j], mv[:, j, 0:1], rstd[:, j:j + 1], ALU.subtract, ALU.mult
                                  ).then_inc(s["v_q"], 1)
            dve.wait_ge(s["ld_gate"], 96)
            dve.tensor_tensor(wc[0:64], wg[0:64, 1], wg[0:64, 2], ALU.add).then_inc(s["v_wc"], 1)
            for b in range(2):
                dve.tensor_tensor(wc[64:128, b], wg[64:128, 1, 1 - b], wg[64:128, 2, 1 - b], ALU.add
                                  ).then_inc(s["v_wc"], 1)
            dve.tensor_copy(wq[0:64, :, :], wg[0:64, 0, :, :]).then_inc(s["v_wq"], 1)
            for b in range(2):
                dve.tensor_copy(wq[64:128, b, :], wg[64:128, 0, 1 - b, :]).then_inc(s["v_wq"], 1)
            dve.wait_ge(s["ld_ctx"], 48)
            dve.tensor_reduce(vsum[:].rearrange("p j h -> p (j h)"), cx.rearrange("p j (h d) -> p (j h) d", d=DH),
                              axis=AX.X, op=ALU.add).then_inc(s["v_vsum"], 1)

            dve.wait_ge(s["t_gates"], NT)
            dve.tensor_tensor(gates[:], ps[:, 4, 0:128].rearrange("p (j g) -> p j g", g=16),
                              gbias[:, None, :].to_broadcast([128, NT, 16]), ALU.add).then_inc(s["v_gates"], 1)
            dve.wait_ge(s["v_gates"], 1)
            dve.scalar_tensor_tensor(out=absf[:], in0=gates[:, :, 0:8], scalar=-1.0, in1=gates[:, :, 0:8],
                                     op0=ALU.mult, op1=ALU.max).then_inc(s["v_absf"], 1)
            dve.wait_ge(s["v_vsum"], 1)
            dve.wait_ge(s["c_v2zero"], 3)
            dve.tensor_scalar(v2[0:64, :, :, 0, DH + 1], vsum[0:64], 1.0 / DH, None, ALU.mult
                              ).then_inc(s["v_vsum"], 1)
            for g in range(2):
                dve.tensor_scalar(v2[64:128, :, 4 * g:4 * g + 4, 1, DH + 1], vsum[64:128, :, 4 - 4 * g:8 - 4 * g],
                                  1.0 / DH, None, ALU.mult).then_inc(s["v_vsum"], 1)
            dve.wait_ge(s["a_ln"], 1)
            dve.scalar_tensor_tensor(out=logf[:], in0=gates[:, :, 0:8], scalar=0.0, in1=lnf[:], op0=ALU.min,
                                     op1=ALU.subtract).then_inc(s["v_logf"], 1)
            dve.wait_ge(s["c_masks"], 3)
            dve.tensor_reduce(h8[:], head_of_row[:], axis=AX.X, op=ALU.add).then_inc(s["v_h8"], 1)
            dve.wait_ge(s["t_cs"], 1)
            for b in range(2):
                rows = slice(64 * b, 64 * b + 64)
                dve.tensor_tensor(a_blk[rows, b].rearrange("p (j h) -> p j h", h=NH), gates[rows, :, 8:16],
                                  ps[rows, 5, 0:64].rearrange("p (j h) -> p j h", h=NH), ALU.subtract
                                  ).then_inc(s["v_a"], 1)
            dve.wait_ge(s["v_a"], 2)
            for b in range(2):
                rows = slice(64 * b, 64 * b + 64)
                dve.tensor_copy(a_hi[rows, :], a_blk[rows, b]).then_inc(s["v_ahl"], 1)
            dve.wait_ge(s["v_ahl"], 2)
            for b in range(2):
                rows = slice(64 * b, 64 * b + 64)
                dve.tensor_tensor(a_lo[rows, :], a_blk[rows, b], a_hi[rows, :].bitcast(F32), ALU.subtract
                                  ).then_inc(s["v_ahl"], 1)
            dve.wait_ge(s["v_small"], 1)
            dve.wait_ge(s["t_at"], 1)
            dve.tensor_tensor_scan(out=top_a[:], data0=zeros[:], data1=ps[:, 0, 0:64], initial=LOWEST,
                                   op0=ALU.add, op1=ALU.max).then_inc(s["v_scan"], 1)
            dve.wait_ge(s["v_scan"], 1)
            k.then(dve.tensor_copy(top_hi[:], top_a[:]))
            k.then(dve.tensor_tensor(top_lo[:], top_a[:], top_hi[:].bitcast(F32), ALU.subtract))
            dve.wait_ge(s["v_h8"], 1)
            for src, dst in ((top_hi, topx_hi), (top_lo, topx_lo)):
                dve.scalar_tensor_tensor(out=dst[:], in0=src[:, None, :].bitcast(F32).to_broadcast([128, NH, S]),
                                         scalar=-1.0, in1=h8[:, :, None].to_broadcast([128, NH, S]),
                                         op0=ALU.mult, op1=ALU.mult).then_inc(s["v_topx"], 1)
            dve.wait_ge(s["t_ct"], 1)
            dve.tensor_tensor(m_full[:], ps[:, 1, 0:64], top_a[:], ALU.add).then_inc(s["v_m"], 1)

            def weigh(j):
                dve.wait_ge(s["t_qk"], j + 1)
                dve.wait_ge(s["a_dec"], j + 1)
                if j >= 2:
                    dve.wait_ge(s["t_pv"], j - 1)
                dve.tensor_tensor(cmat[:, j % 2].rearrange("p h s -> p (h s)"), ps[:, SCORE_BANK[j], :],
                                  dec[:, j % 2, :], ALU.mult).then_inc(s["v_c"], 1)

            def w_high(e, slot):
                if not (isinstance(e, int) and e < 2):
                    dve.wait_ge(s["t_down"], FC * e - FC)
                dve.tensor_scalar(b1_now[:, slot, :], vecs_t[:, bass.ds(FC * e, FC)], 1.0, None, ALU.mult
                                  ).then_inc(s["v_b1"], 1)
                dve.wait_ge(ld_raw[slot], e_loaded(e, slot))
                dve.tensor_scalar(w_hi[:, slot, :], raw[:, slot, :], 1.0, None, ALU.mult).then_inc(s["v_whi"], 1)

            def e_loaded(e, slot):
                return (e - slot) * 16 + 32

            def heads_centre(half):
                u = u_half(half)
                sums = u[:, :, :, DH]
                v = lambda t: t[:, half].rearrange("p (j c) -> p j c", j=2)
                dve.wait_ge(s["t_pv"], 4 * (half + 1))
                dve.wait_ge(s["a_em"], 1)
                emv = em[:, 2 * half:2 * half + 2].rearrange("p j b h -> p j (b h)")
                k.mark(dve.tensor_copy(v(hmean), u[:, :, :, DH + 1]))
                k.then(dve.scalar_tensor_tensor(out=v(t1), in0=sums, scalar=-1.0, in1=emv,
                                                op0=ALU.mult, op1=ALU.max))
                k.mark(dve.tensor_tensor(v(nrm), sums, v(t1), ALU.max))
                ucv = uc[:, half].rearrange("p (j c d) -> p j c d", j=2, d=DH)
                dve.tensor_tensor(ucv, u[:, :, :, 0:DH], v(hmean)[:, :, :, None].to_broadcast([128, 2, 16, DH]),
                                  ALU.subtract).then_inc(s["v_uc"], 1)
                k.wait()
                k.then(dve.tensor_scalar(nrm[:, half], nrm[:, half], 1e-6, None, ALU.add))
                k.then(dve.reciprocal(rn[:, half], nrm[:, half]))
                k.mark(dve.tensor_tensor(rn2[:, half], rn[:, half], rn[:, half], ALU.mult))

            def heads_norm(half, guess):
                u = 1 + half
                dve.wait_ge(s["v_uc"], half + 1)
                dve.wait_ge(s["a_usq"], half + 1)
                k.then(dve.tensor_reduce(v16[:, half], usq[:, half].rearrange("p (c d) -> p c d", d=DH), axis=AX.X,
                                         op=ALU.add))
                k.then(dve.tensor_tensor(hv[:, half], v16[:, half], rn2[:, half], ALU.mult))
                dve.tensor_scalar(rs_in[:, u, :], hv[:, half], 1.0 / DH, 1e-6, ALU.mult, ALU.add
                                  ).then_inc(s["v_rs"], 1)
                dve.wait_ge(s["v_rs"], RS_WRITTEN[guess])
                rsqrt_begin(u, 32)

            def heads_scale(half, guess):
                rsqrt_end(1 + half, 32, guess, hf[:, half], rn[:, half])
                dve.wait_ge(s["v_newton"], guess)
                dve.wait_ge(s["p_ucw"], half + 1)
                h4 = slice(4 * half, 4 * half + 4)
                dve.tensor_tensor(att[:, h4].rearrange("p t (h d) -> p (t h) d", d=DH),
                                  ucw[:, h4].rearrange("p t (h d) -> p (t h) d", d=DH),
                                  hf[:, half, :, None].to_broadcast([128, 32, DH]), ALU.mult
                                  ).then_inc(s["v_att"], 1)

            def second_heads_add():
                dve.wait_ge(s["ld_x2"], 32)
                dve.wait_ge(s["v_att"], 2)
                k.then(dve.tensor_tensor(x_mid[:, 4:8], att[:, 4:8], x2[:, 4:8], ALU.add))

            def tile_stats(half, st, out, src, sem_v):
                for i in range(4):
                    dve.bn_stats(st[:, 4 * half + i], src[i]).then_inc(sem_v, 1)
                for i in range(4):
                    t = 4 * half + i
                    dve.wait_ge(sem_v, 8 * half + i + 1)
                    dve.bn_aggr(out[:, t], st[:, t]).then_inc(sem_v, 1)
                dve.wait_ge(sem_v, 8 * half + 8)

            def norms_stats(half, guess):
                h4, u = slice(4 * half, 4 * half + 4), 3 + half
                tile_stats(half, st1, mv1, [x_mid[:, t] for t in range(4 * half, 4 * half + 4)], s["v_mv1"])
                dve.tensor_scalar(rs_in[:, u, 0:4], mv1[:, h4, 1], 1e-5, None, ALU.add).then_inc(s["v_rs"], 1)
                dve.tensor_scalar(rs_in[:, u, 4:8], mv1[:, h4, 1], 1.0 + 1e-5, 1e-10, ALU.mult, ALU.add
                                  ).then_inc(s["v_rs"], 1)
                dve.wait_ge(s["v_rs"], RS_WRITTEN[guess])
                rsqrt_begin(u, 8)

            def norms_out(half, guess):
                rsqrt_end(3 + half, 8, guess, r1[:, half].rearrange("p a t -> p (a t)"))
                dve.wait_ge(s["v_newton"], guess)
                m = mv1[:, None, 4 * half:4 * half + 4, 0].to_broadcast([128, 2, 4])
                dve.scalar_tensor_tensor(out=mr1[:, half], in0=m, scalar=-1.0, in1=r1[:, half],
                                         op0=ALU.mult, op1=ALU.mult).then_inc(s["v_mr1"], 1)
                if half == 1:
                    for i in range(2, 4):
                        t = 4 * half + i
                        dve.tensor_scalar(nrow[:, t], x_mid[:, t], mv1[:, t, 0:1], r1[:, half, 1, i:i + 1],
                                          ALU.subtract, ALU.mult).then_inc(s["v_nrow"], 1)

            def mixed_stats(half, guess):
                h4, u = slice(4 * half, 4 * half + 4), 5 + half
                dve.wait_ge(s["t_z"], half + 1)
                tile_stats(half, st2, mv2, [z_tile(t) for t in range(4 * half, 4 * half + 4)], s["v_mv2"])
                dve.tensor_scalar(rs_in[:, u, 0:4], mv2[:, h4, 1], 1e-5, None, ALU.add).then_inc(s["v_rs"], 1)
                dve.wait_ge(s["v_rs"], RS_WRITTEN[guess])
                rsqrt_begin(u, 4)

            def mixed_out(half, guess):
                h4 = slice(4 * half, 4 * half + 4)
                rsqrt_end(5 + half, 4, guess, r2[:, h4])
                dve.wait_ge(s["v_newton"], guess)
                dve.scalar_tensor_tensor(out=mr2[:, h4], in0=mv2[:, h4, 0], scalar=-1.0, in1=r2[:, h4],
                                         op0=ALU.mult, op1=ALU.mult).then_inc(s["v_mr2"], 1)
                if half == 1:
                    for t in (6, 7):
                        dve.tensor_scalar(zn[:, t], z_tile(t), mv2[:, t, 0:1], r2[:, t:t + 1],
                                          ALU.subtract, ALU.mult).then_inc(s["v_zn"], 1)

            def residual(half):
                h4 = slice(4 * half, 4 * half + 4)
                dve.wait_ge(s["a_zn"], 4 + 2 * half)
                pairs = lambda v: v[:, h4].rearrange("p (a i) e -> p a (i e)", a=2)
                z = ps[:, 2:4, 0:256] if half else ps[:, 5, :].rearrange("p (a n) -> p a n", a=2)
                dve.tensor_tensor(pairs(base), z, pairs(x_mid), ALU.add).then_inc(s["v_base"], 1)

            def low_n2(half):
                cols = slice(512 * half, 512 * half + 512)
                dve.wait_ge(s["a_n2"], 2 * half + 2)
                dve.tensor_tensor(n2_lo[:, cols], n2[:, cols], n2_hi[:, cols].bitcast(F32), ALU.subtract
                                  ).then_inc(s["v_n2lo"], 1)

            dve.wait_ge(s["ld_mix"], 32)
            dve.wait_ge(s["c_ident"], 1)
            dve.tensor_tensor(mixw[:], mixw[:], ident[:], ALU.add).then_inc(s["v_mixw"], 1)
            weigh(0)
            weigh(1)
            q_diag(dve, 4, s["v_qd"])
            dve.wait_ge(s["a_vecs"], 1)
            w_high(0, 0)
            weigh(2)
            q_diag(dve, 5, s["v_qd"])
            w_high(1, 1)
            weigh(3)
            q_diag(dve, 6, s["v_qd"])
            weigh(4)
            heads_centre(0)
            weigh(5)
            heads_norm(0, 2)
            heads_scale(0, 2)
            weigh(6)
            weigh(7)
            dve.wait_ge(s["p_xmid"], 1)
            norms_stats(0, 3)
            heads_centre(1)
            heads_norm(1, 4)
            norms_out(0, 3)
            heads_scale(1, 4)
            second_heads_add()
            norms_stats(1, 5)
            norms_out(1, 5)
            mixed_stats(0, 6)
            mixed_out(0, 6)
            mixed_stats(1, 7)
            mixed_out(1, 7)
            low_n2(0)
            residual(1)

            def h_low(g_base, g):
                n = g_base + g
                dve.wait_ge(s["a_hi"], n + 1)
                if not (isinstance(g_base, int) and n < 4):
                    dve.wait_ge(s["t_down"], n - 3)
                dve.tensor_tensor(h_lo[:, g % 4, :], h_f[:, g % 2, :], h_hi[:, g % 4, :].bitcast(F32),
                                  ALU.subtract).then_inc(s["v_lo"], 1)

            logits = ps[:, 6, 0:64].rearrange("p (t e) -> p t e", e=NX)
            wide = lambda n: rsm[:, n, :, None].to_broadcast([128, NT, NX])
            dve.wait_ge(s["t_router"], NT)
            dve.tensor_reduce(rsm[:, 0], logits, axis=AX.X, op=ALU.max).then_inc(s["v_rt"], 1)
            dve.wait_ge(s["v_rt"], 1)
            dve.tensor_tensor(rt[:, 0], logits, wide(0), ALU.subtract).then_inc(s["v_rt"], 1)
            low_n2(1)
            residual(0)
            dve.wait_ge(s["a_rexp"], 1)
            k.then(dve.tensor_reduce(rsm[:, 1], rt[:, 1], axis=AX.X, op=ALU.add))
            k.then(dve.reciprocal(rsm[:, 2], rsm[:, 1]))
            k.then(dve.tensor_tensor(rt[:, 2], rt[:, 1], wide(2), ALU.mult))
            rank_b = rank[:, None, :].to_broadcast([128, NT, NX])

            def first_low(half, sem_hi, sem_lo):
                cols = slice(512 * half, 512 * half + 512)
                dve.wait_ge(sem_hi, 1)
                dve.tensor_tensor(h_lo[:, 0, cols], h_f[:, 0, cols], h_hi[:, 0, cols].bitcast(F32),
                                  ALU.subtract).then_inc(sem_lo, 1)

            def first_largest(prob, mx, same, ranked, best, onehot):
                k.then(dve.tensor_reduce(rsm[:, mx], rt[:, prob], axis=AX.X, op=ALU.max))
                k.then(dve.tensor_tensor(rt[:, same], rt[:, prob], wide(mx), ALU.is_equal))
                k.then(dve.tensor_tensor(rt[:, ranked], rt[:, same], rank_b, ALU.mult))
                if prob == 2:
                    first_low(0, s["a_first"], s["v_first"])
                k.then(dve.tensor_reduce(rsm[:, best], rt[:, ranked], axis=AX.X, op=ALU.max))
                k.then(dve.tensor_tensor(rt[:, onehot], rt[:, ranked], wide(best), ALU.is_equal))

            first_largest(2, 3, 3, 4, 4, 5)
            k.then(dve.scalar_tensor_tensor(out=rt[:, 6], in0=rt[:, 5], scalar=-4.0, in1=rt[:, 2],
                                            op0=ALU.mult, op1=ALU.add))
            first_low(1, s["a_hi"], s["v_lo"])
            first_largest(6, 5, 7, 8, 6, 9)
            k.then(dve.tensor_tensor(rt[:, 10], rt[:, 5], rt[:, 9], ALU.add))
            dve.tensor_tensor(comb[:], rt[:, 10], rt[:, 2], ALU.mult).then_inc(s["v_comb"], 1)

            def weigh_y(e, slot, dst=part):
                bank = 6 - 2 * slot
                dve.wait_ge(s["t_down"], 4 * e + 4)
                if dst is part:
                    dve.wait_ge(s["v_comb_e"], 2 * e)
                dve.scalar_tensor_tensor(out=dst, in0=ps[:, bank:bank + 2, :].rearrange("p a n -> p (a n)"),
                                         scalar=vecs_t[:, bass.ds(B2_AT + e, 1)],
                                         in1=comb_all[:, bass.ds(e, 1), :].squeeze(1), op0=ALU.add, op1=ALU.mult
                                         ).then_inc(s["v_comb_e"], 1 if dst is part else 2)

            def add_y(e):
                dve.wait_ge(s["v_comb_e"], 2 * e + 1)
                dve.tensor_tensor(acc, part, acc, ALU.add).then_inc(s["v_comb_e"], 1)

            for g in range(1, 4):
                h_low(0, g)
            for half in range(2):
                dve.wait_ge(s["t_combt"], 4 * (half + 1))
                dve.tensor_copy(comb_t[:, 512 * half:512 * half + 512], ps[0:NX, 4 + half, :]
                                ).then_inc(s["v_combt"], 1)
            h_low(0, 4)
            w_high(2, 0)
            h_low(0, 5)
            h_low(0, 6)
            dve.wait_ge(s["comb_first"], 16)
            weigh_y(0, 0, acc)
            h_low(0, 7)
            with dve.Fori(1, NX // 2 - 1) as i:
                for u in range(2):
                    h_low(8 * i, 4 * u)
                    w_high(2 * i + u + 1, 1 - u)
                    if u == 1:
                        dve.wait_ge(s["comb_rest"], 16)
                    weigh_y(2 * i + u - 1, 1 - u)
                    h_low(8 * i, 4 * u + 1)
                    add_y(2 * i + u - 1)
                    h_low(8 * i, 4 * u + 2)
                    h_low(8 * i, 4 * u + 3)
            last = NX - 2
            for u in range(2):
                h_low(4 * last, 4 * u)
                if u == 0:
                    w_high(last + 1, 1)
                weigh_y(last + u - 1, 1 - u)
                h_low(4 * last, 4 * u + 1)
                add_y(last + u - 1)
                h_low(4 * last, 4 * u + 2)
                if u == 0:
                    h_low(4 * last, 3)
            dve.wait_ge(s["t_down"], LAST - 3)
            for half in range(2):
                cols = slice(512 * half, 512 * half + 512)
                dve.wait_ge(s["a_hi"], LAST + 1 + half)
                dve.tensor_tensor(h_lo[:, 3, cols], h_f[:, 1, cols], h_hi[:, 3, cols].bitcast(F32),
                                  ALU.subtract).then_inc(s["v_lo"], 1)

            def base_add(half):
                h4 = slice(4 * half, 4 * half + 4)
                dve.wait_ge(s["v_base"], 2 + half)
                dve.wait_ge(s["t_acc"], half + 1)
                dve.tensor_tensor(base[:, h4], ps[:, 6 + half, :].rearrange("p (t e) -> p t e", e=E), base[:, h4],
                                  ALU.add).then_inc(s["v_base"], 1)

            def result(half):
                h4 = slice(4 * half, 4 * half + 4)
                dve.wait_ge(s["v_base"], 3 + half)
                dve.wait_ge(s["t_fin"], half + 1)
                dve.tensor_tensor(fin[:, h4], ps[:, 2 + half, :].rearrange("p (t e) -> p t e", e=E), base[:, h4],
                                  ALU.add).then_inc(s["v_fin"], 1)

            base_add(0)
            dve.wait_ge(s["v_comb_e"], 2 * NX - 2)
            for half in range(2):
                cols = slice(512 * half, 512 * half + 512)
                dve.wait_ge(s["t_down"], LAST + 1 + half)
                dve.scalar_tensor_tensor(out=part[:, cols], in0=ps[:, 4 + half, :],
                                         scalar=vecs_t[:, B2_AT + NX - 1:B2_AT + NX],
                                         in1=comb_all[:, NX - 1, cols], op0=ALU.add, op1=ALU.mult
                                         ).then_inc(s["v_comb_e"], 1)
            result(0)
            base_add(1)
            result(1)

        @blk.tensor
        def _(pe):
            def keep_busy(n, bank):
                for _ in range(n):
                    pe.matmul(ps[:, bank, :], ident_bf[:], ident_bf[:, None, :].to_broadcast([128, 4, 128]),
                              start=True, stop=True)

            pe.wait_ge(s["a_id"], 2)
            keep_busy(FILL_START, 7)
            pe.wait_ge(s["c_ident"], 1)
            pe.wait_ge(s["ld_ctx"], 48)
            for j in range(NT):
                pe.transpose(ps[:, 2 + j // 4, 128 * (j % 4):128 * (j % 4) + 128], cx[:, j], ident[:]
                             ).then_inc(s["t_ctx"], 1)
            for j in range(NT):
                if j < QN_BY_ACT:
                    pe.wait_ge(s["v_q"], j + 1)
                else:
                    pe.wait_ge(s["a_qn"], j + 1 - QN_BY_ACT)
                pe.transpose(ps[:, j // 4, 128 * (j % 4):128 * (j % 4) + 128], qn[:, j], ident[:]
                             ).then_inc(s["t_q"], 1)

            def gate_part(rows, w, j, first):
                for b in range(2):
                    m = pe.matmul(ps[64 * b:64 * b + 64, 4, 16 * j:16 * j + 16], rows[:, j, b], w[:, b],
                                  start=first and j == 0, stop=True, skip_group_check=True)
                return m

            pe.wait_ge(s["v_wc"], 3)
            for j in range(NT):
                if j % 4 == 0:
                    pe.wait_ge(s["a_ct"], j // 4 + 1)
                gate_part(c_t, wc, j, True)
            pe.wait_ge(s["v_wq"], 3)
            for j in range(NT):
                if j % 4 == 0:
                    pe.wait_ge(s["a_q"], j // 4 + 1)
                gate_part(q_t, wq, j, False).then_inc(s["t_gates"], 1)

            def scores(n):
                j = ORDER[n]
                pe.wait_ge(s["p_qd"] if n in BY_POOL else s["v_qd"], 4 * (spread_before(n) + 1))
                bank = SCORE_BANK[n]
                if bank in SCORE_BANK[:n]:
                    pe.wait_ge(s["v_c"], max(m for m in range(n) if SCORE_BANK[m] == bank) + 1)
                for g in range(2):
                    m = pe.matmul(ps[:, bank, 256 * g:256 * g + 256], k_m[:, j, g].rearrange("p b t -> p (b t)"),
                                  qd[:, n % 4, g].rearrange("p h s -> p (h s)"), start=True, stop=True)
                m.then_inc(s["t_qk"], 1)

            def log_decay(n):
                j = ORDER[n]
                o = ps[:, n % 2, :]
                if n >= 2:
                    pe.wait_ge(s["a_dec"], n - 1)
                pk = pick_r[:, j].rearrange("p b t -> p (b t)")
                wide_a = lambda t: t[:, NH * j:NH * j + NH, None].to_broadcast([128, NH, S])
                pe.matmul(o, ident_r[:], wide_a(a_hi), start=True, stop=False)
                pe.matmul(o, ident_r[:], wide_a(a_lo), start=False, stop=False)
                pe.matmul(o, ident_bf[:], later_bf[:, None, :].to_broadcast([128, NH, S]), start=False, stop=False)
                if n == 0:
                    pe.wait_ge(s["v_topx"], 2)
                pe.matmul(o, pk, topx_hi[:].rearrange("p h s -> p (h s)"), start=False, stop=False)
                pe.matmul(o, pk, topx_lo[:].rearrange("p h s -> p (h s)"), start=False, stop=True
                          ).then_inc(s["t_l"], 1)

            def values(n):
                j = ORDER[n]
                jp, jh = j // 4, j % 4
                pe.wait_ge(s["v_c"], n + 1)
                for h in range(NH):
                    o = ps[64 * jp:64 * jp + 64, 4 + jh, 0:2 * NH * UW].rearrange(
                        "p (b h d) -> p b h d", b=2, h=NH)[:, :, h, :]
                    m = pe.matmul(o, cmat[:, n % 2, h], v2[:, j, h], start=True, stop=True)
                m.then_inc(s["t_pv"], 1)

            pe.wait_ge(s["a_k"], 4)
            scores(0)
            pe.wait_ge(s["v_logf"], 1)
            pe.wait_ge(s["c_small"], 3)
            pe.matmul(ps[:, 5, 0:64], tri[:], logf[:].rearrange("p j h -> p (j h)"), start=True, stop=True
                      ).then_inc(s["t_cs"], 1)
            keep_busy(FILL_SUMS, 7)
            pe.wait_ge(s["ld_vecs"], 96)
            pe.transpose(ps[:, 1, 256:256 + NVEC], vecs[:], ident[0:NVEC, 0:NVEC]).then_inc(s["t_vecs"], 1)
            pe.wait_ge(s["v_a"], 2)
            pe.matmul(ps[:, 0, 0:64], a_blk[:].rearrange("p b c -> p (b c)"), eye2[:], start=True, stop=True
                      ).then_inc(s["t_at"], 1)
            pe.wait_ge(s["a_k"], 8)
            scores(1)
            pe.wait_ge(s["a_cblk"], 2)
            pe.wait_ge(s["a_vecs"], 1)
            pe.matmul(ps[:, 1, 0:64], c_blk[:].rearrange("p b c -> p (b c)"), eye2[:], start=True, stop=True
                      ).then_inc(s["t_ct"], 1)
            pe.wait_ge(s["v_ahl"], 4)
            pe.wait_ge(s["a_id"], 3)
            pe.wait_ge(s["c_masks"], 3)
            pe.wait_ge(s["v_scan"], 1)
            log_decay(0)
            scores(2)
            pe.wait_ge(s["v_m"], 1)
            iv = ident[:].rearrange("p (b jp jh h) -> p jp b jh h", b=2, jh=4, jp=2)
            for jp in range(2):
                pe.matmul(ps[64 * jp:64 * jp + 64, 5, 64:128], m_full[:], iv[:, jp], start=True, stop=True
                          ).then_inc(s["t_em"], 1)
            log_decay(1)
            pe.wait_ge(s["a_v2"], 3)
            pe.wait_ge(s["v_vsum"], 4)
            for n in range(NT):
                if n == 2:
                    pe.wait_ge(s["a_em"], 1)
                values(n)
                if n < 3:
                    scores(n + 3)
                elif n in (4, 5):
                    scores(n + 2)
                if n + 2 < NT:
                    log_decay(n + 2)

            def token_tile(t):
                return slice(128 * (t % 4), 128 * (t % 4) + 128)

            def transpose_tiles(half, src, by_act, by_dve, sem_t, fill=0):
                for i in range(4):
                    if half == 0 or i < 2:
                        pe.wait_ge(by_act, 4 * half + i + 1)
                    else:
                        pe.wait_ge(by_dve, i - 1)
                    pe.transpose(ps[:, T_BANK[half], token_tile(i)], src[:, 4 * half + i], ident[:]
                                 ).then_inc(sem_t, 1)
                    keep_busy(fill, 1)

            def mix_bias(half):
                for o in ([ps[:, 5, :]] if half == 0 else [ps[:, 2, 0:256], ps[:, 3, 0:256]]):
                    pe.matmul(o, ones_row[:], mixb[:, None, :].to_broadcast([1, o.shape[-1] // E, E]), start=True,
                              stop=False, skip_group_check=True)

            def mix(half):
                tiles = range(4 * half, 4 * half + 4)
                for t in tiles:
                    pe.wait_ge(s["p_y0"], t + 1)
                    pe.matmul(z_tile(t), ident[:], y0[:, t], start=False, stop=False,
                              skip_group_check=True)
                pe.wait_ge(s["a_nt"], half + 1)
                for t in tiles:
                    m = pe.matmul(z_tile(t), n_t[:, 128 * t:128 * t + 128], mixw[:], start=False,
                                  stop=True, skip_group_check=True)
                m.then_inc(s["t_z"], 1)

            def route(half):
                pe.wait_ge(s["a_n2"], 2 * half + 1)
                for t in range(4 * half, 4 * half + 4):
                    pe.matmul(ps[:, 6, NX * t:NX * t + NX], n2[:, 128 * t:128 * t + 128], rw[:], start=True,
                              stop=True).then_inc(s["t_router"], 1)

            def up_half(hi, lo, bank, half):
                o = ps[:, bank + half, :]
                cols = slice(512 * half, 512 * half + 512)
                pe.matmul(o, hi, n2_hi[:, cols], start=True, stop=False)
                pe.matmul(o, lo, n2_hi[:, cols], start=False, stop=False)
                return pe.matmul(o, hi, n2_lo[:, cols], start=False, stop=True)

            def w1_parts(slot, c):
                return w_hi[:, slot, 128 * c:128 * c + 128], w_lo[:, slot, 128 * c:128 * c + 128]

            pe.wait_ge(s["v_uc"], 1)
            pe.wait_ge(s["v_mixw"], 1)
            pe.wait_ge(s["a_dec"], NT)
            pe.wait_ge(s["v_c"], NT)
            keep_busy(FILL_HEADS, 1)
            pe.wait_ge(s["v_small"], 3)
            mix_bias(0)
            transpose_tiles(0, nrow, s["a_nrow"], s["v_nrow"], s["t_nrow"], fill=FILL_NORMS)
            mix(0)
            mix_bias(1)
            pe.wait_ge(s["v_uc"], 2)
            transpose_tiles(1, nrow, s["a_nrow"], s["v_nrow"], s["t_nrow"])
            mix(1)
            transpose_tiles(0, zn, s["a_zn"], s["v_zn"], s["t_n2"], fill=FILL_Z)
            keep_busy(FILL_ROUTE, 1)
            pe.wait_ge(s["ld_rw"], 16)
            route(0)
            transpose_tiles(1, zn, s["a_zn"], s["v_zn"], s["t_n2"])
            keep_busy(FILL_UP, 1)
            route(1)
            pe.wait_ge(s["v_whi"], 1)
            pe.wait_ge(s["p_wlo"], 1)
            pe.wait_ge(s["v_n2lo"], 1)
            up_half(*w1_parts(0, 0), 0, 0).then_inc(s["t_first"], 1)
            pe.wait_ge(s["v_base"], 1)
            up_half(*w1_parts(0, 1), 2, 0)
            pe.wait_ge(s["a_n2"], 4)
            pe.wait_ge(s["v_n2lo"], 2)
            for c in range(2):
                up_half(*w1_parts(0, c), 2 * c, 1).then_inc(s["t_up"], 1)

            def up(g_base, g):
                n = g_base + g
                slot, c = (g // FC) % 2, g % FC
                if g % FC == 0:
                    if isinstance(n, int):
                        e1 = n // FC + 1
                        pe.wait_ge(s["v_whi"], e1)
                        pe.wait_ge(s["p_wlo"], e1)
                bank = up_bank(g)
                if isinstance(n, int) and n == EARLY:
                    bank = 4
                    pe.wait_ge(s["a_n2"], 2)
                    pe.wait_ge(s["v_base"], 2)
                elif isinstance(n, int) and n <= EARLY + 2:
                    pe.wait_ge(s["a_hi"], n - 2)
                else:
                    pe.wait_ge(s["a_hi"], n - 1)
                for half in range(2):
                    m = up_half(*w1_parts(slot, c), bank, half)
                    if half or (isinstance(n, int) and n == LAST):
                        m.then_inc(s["t_up"], 1)

            def down_half(slot, c, g, half):
                hi = w_hi[:, slot, F + 128 * c:F + 128 * c + 128]
                lo = w_lo[:, slot, F + 128 * c:F + 128 * c + 128]
                o = ps[:, 6 - 2 * slot + half, :]
                cols = slice(512 * half, 512 * half + 512)
                pe.matmul(o, hi, h_hi[:, g % 4, cols], start=(c == 0), stop=False)
                pe.matmul(o, lo, h_hi[:, g % 4, cols], start=False, stop=False)
                return pe.matmul(o, hi, h_lo[:, g % 4, cols], start=False, stop=(c == FC - 1))

            def down(g_base, g):
                n = g_base + g
                last = isinstance(n, int) and n == LAST
                if not last:
                    pe.wait_ge(s["v_lo"], n + 1)
                for half in range(2):
                    if last:
                        pe.wait_ge(s["v_lo"], n + 1 + half)
                    m = down_half((g // FC) % 2, g % FC, g, half)
                    if half or last:
                        m.then_inc(s["t_down"], 1)

            up(0, EARLY)

            def combine_t():
                pe.wait_ge(s["a_hi"], EARLY + 1)
                pe.wait_ge(s["v_comb"], 1)
                for t in range(NT):
                    pe.transpose(ps[0:NX, 4 + t // 4, token_tile(t)], comb[:, t], ident[:]).then_inc(s["t_combt"], 1)

            def turn(g_base, g):
                if not (isinstance(g_base, int) and g_base + g + 2 > LAST):
                    if (g + 2) % FC == 0 and not isinstance(g_base, int):
                        e1 = 2 * expert_pair + (g + 2) // FC + 1
                        pe.wait_ge(s["v_whi"], e1)
                        pe.wait_ge(s["p_wlo"], e1)
                    up(g_base, g + 2)
                if g == FC and isinstance(g_base, int) and g_base == 0:
                    pe.wait_ge(s["v_combt"], 2)
                elif g % FC == 0:
                    if isinstance(g_base, int):
                        done = 2 * ((g_base + g) // FC - 2) + 1
                    else:
                        done = 4 * expert_pair + 2 * (g // FC) - 3
                    pe.wait_ge(s["v_comb_e"], done)
                down(g_base, g)

            pe.wait_ge(s["v_first"], 1)
            down_half(0, 0, 0, 0)
            up(0, EARLY + 1)
            pe.wait_ge(s["v_lo"], 1)
            down_half(0, 0, 0, 1).then_inc(s["t_down"], 1)
            up(0, EARLY + 2)
            down(0, 1)
            down(0, 2)
            combine_t()
            for g in range(3, 8):
                turn(0, g)
            with pe.Fori(1, NX // 2 - 1) as expert_pair:
                for g in range(8):
                    turn(8 * expert_pair, g)

            def to_tokens(src, half, bank, done):
                for t in range(4 * half, 4 * half + 4):
                    m = pe.transpose(ps[:, bank, token_tile(t)], src[:, 128 * t:128 * t + 128], ident[:])
                m.then_inc(done, 1)

            for g in range(7):
                turn(NX * FC - 8, g)
            pe.wait_ge(s["v_comb_e"], 2 * NX - 2)
            to_tokens(acc, 0, 6, s["t_acc"])
            turn(NX * FC - 8, 7)
            to_tokens(acc, 1, 7, s["t_acc"])
            for half in range(2):
                pe.wait_ge(s["v_comb_e"], 2 * NX - 1 + half)
                to_tokens(part, half, 2 + half, s["t_fin"])


INPUTS = ["x", "ctx_1024", "L0_xattn_igate_kernel", "L0_xattn_igate_bias", "L0_xattn_fgate_kernel",
          "L0_xattn_fgate_bias", "L0_xattn_outnorm_weight", "L0_ffn_g1", "L0_ffn_be1", "L0_ffn_mix_w",
          "L0_ffn_mix_b", "L0_ffn_g2", "L0_ffn_be2", "L0_ffn_router_w", "L0_ffn_w1", "L0_ffn_b1",
          "L0_ffn_w2", "L0_ffn_b2"]


def kernel(**inputs):
    import numpy as np
    import concourse.bacc as bacc
    from concourse.bass_utils import run_bass_kernel_spmd

    nc = bacc.Bacc("TRN2", target_bir_lowering=False, num_devices=1)
    arrays, args = {}, []
    for name in INPUTS:
        a = np.ascontiguousarray(inputs[name])
        arrays[f"in_{name}"] = a
        args.append(nc.dram_tensor(f"in_{name}", a.shape, mybir.dt.from_np(a.dtype), kind="ExternalInput").ap())
    out = nc.dram_tensor("out", (B, S, E), F32, kind="ExternalOutput").ap()
    build(nc, *args, out)
    r = run_bass_kernel_spmd(nc, [arrays], core_ids=[0])
    return r.results[0]["out"]
```
